# Optimizing a Trainium2 kernel written in Bass

```python
import numpy as np
import jax
import jax.numpy as jnp

def _softmax(x, axis=-1):
    return jax.nn.softmax(x, axis=axis)

def _gelu(x):
    return jax.nn.gelu(x, approximate=True)

def _silu(x):
    return jax.nn.silu(x)

def _sigmoid(x):
    return jax.nn.sigmoid(x)

def _layernorm(x, axis=-1, eps=1e-05):
    m = jnp.mean(x, axis=axis, keepdims=True)
    v = jnp.var(x, axis=axis, keepdims=True)
    return (x - m) / jnp.sqrt(v + eps)

def _scatter_add(tgt, idx, src, axis=0):
    return tgt.at[idx].add(src)

def _segment_sum(src, seg, n):
    return jax.ops.segment_sum(src, seg, n)
kernel_name = 'mk_seq_preln_d2_jaxref_r8_5db1d4'

def setup_inputs(seed: int=0):
    np.random.seed(seed)
    _w = jnp.asarray

    def _L0_attn_setup():
        import jax, jax.numpy as jnp
        import numpy as np
        import math
        B, L, E, H = (4, 512, 256, 16)
        HD = E // H
        key = jax.random.key(seed)
        k1, k2, k3, k4, k5 = jax.random.split(key, 5)
        s = 1.0 / math.sqrt(E)
        return {'x': jax.random.normal(k1, (B, L, E), dtype=jnp.float32), 'Wq': jax.random.normal(k2, (E, E), dtype=jnp.float32) * s, 'bq': jax.random.normal(k3, (E,), dtype=jnp.float32) * s, 'Wkv': jax.random.normal(k4, (2 * HD, E), dtype=jnp.float32) * s, 'bkv': jax.random.normal(k5, (2 * HD,), dtype=jnp.float32) * s}
    _L0_attn_in = _L0_attn_setup()

    def _L0_ffn_setup():
        import jax, jax.numpy as jnp
        import numpy as np
        B, S, D, FF, E = (4, 256, 256, 1024, 2)
        key = jax.random.key(seed)
        k0, k1, k2, k3, k4 = jax.random.split(key, 5)
        s = 0.02
        return {'hidden_states': jax.random.normal(k0, (B, S, D), jnp.float32), 'gate_w': jax.random.normal(k1, (E, D), jnp.float32) * s, 'w_gate': jax.random.normal(k2, (E, FF, D), jnp.float32) * s, 'w_up': jax.random.normal(k3, (E, FF, D), jnp.float32) * s, 'w_down': jax.random.normal(k4, (E, D, FF), jnp.float32) * s}
    _L0_ffn_in = _L0_ffn_setup()

    def _L1_attn_setup():
        import jax, jax.numpy as jnp
        import numpy as np
        BSZ, L, D_INNER, D_STATE = (2, 256, 256, 8)
        DT_RANK = D_INNER // 8
        key = jax.random.key(seed)
        k0, k1, k2, k3 = jax.random.split(key, 4)
        x = jax.random.normal(k0, (BSZ, L, D_INNER), jnp.float32)
        W_xproj = jax.random.normal(k1, (DT_RANK + 2 * D_STATE, D_INNER), jnp.float32) * 0.02
        std = DT_RANK ** (-0.5)
        W_dt = jax.random.uniform(k2, (D_INNER, DT_RANK), jnp.float32, -std, std)
        dt = jnp.exp(jax.random.uniform(k3, (D_INNER,), jnp.float32) * (jnp.log(0.1) - jnp.log(0.001)) + jnp.log(0.001))
        dt = jnp.clip(dt, 0.0001)
        b_dt = dt + jnp.log(-jnp.expm1(-dt))
        A_log = jnp.log(jnp.broadcast_to(jnp.arange(1, D_STATE + 1, dtype=jnp.float32), (D_INNER, D_STATE)))
        D_param = jnp.ones((D_INNER,), jnp.float32)
        return {'x': x, 'W_xproj': W_xproj, 'W_dt': W_dt, 'b_dt': b_dt, 'A_log': A_log, 'D_param': D_param}
    _L1_attn_in = _L1_attn_setup()

    def _L1_ffn_setup():
        import jax, jax.numpy as jnp
        import numpy as np
        H = 256
        F = 176
        E = 64
        TOP_K = 6
        CAP = 64
        SCALE = 1.0
        F_SH = 2 * F
        B, S = (1, 256)
        key = jax.random.key(seed)
        ks = jax.random.split(key, 8)
        s = 0.02
        return {'hidden_states': jax.random.normal(ks[0], (B, S, H), jnp.float32), 'gate_w': jax.random.normal(ks[1], (E, H), jnp.float32) * s, 'w_gate': jax.random.normal(ks[2], (E, H, F), jnp.float32) * s, 'w_up': jax.random.normal(ks[3], (E, H, F), jnp.float32) * s, 'w_down': jax.random.normal(ks[4], (E, F, H), jnp.float32) * s, 'sh_gate': jax.random.normal(ks[5], (F_SH, H), jnp.float32) * s, 'sh_up': jax.random.normal(ks[6], (F_SH, H), jnp.float32) * s, 'sh_down': jax.random.normal(ks[7], (H, F_SH), jnp.float32) * s}
    _L1_ffn_in = _L1_ffn_setup()
    _d = {'L0_attn_x': _L0_attn_in['x'], 'L0_attn_Wq': _L0_attn_in['Wq'], 'L0_attn_bq': _L0_attn_in['bq'], 'L0_attn_Wkv': _L0_attn_in['Wkv'], 'L0_attn_bkv': _L0_attn_in['bkv'], 'L0_ffn_gate_w': _L0_ffn_in['gate_w'], 'L0_ffn_w_gate': _L0_ffn_in['w_gate'], 'L0_ffn_w_up': _L0_ffn_in['w_up'], 'L0_ffn_w_down': _L0_ffn_in['w_down'], 'L1_attn_W_xproj': _L1_attn_in['W_xproj'], 'L1_attn_W_dt': _L1_attn_in['W_dt'], 'L1_attn_b_dt': _L1_attn_in['b_dt'], 'L1_attn_A_log': _L1_attn_in['A_log'], 'L1_attn_D_param': _L1_attn_in['D_param'], 'L1_ffn_gate_w': _L1_ffn_in['gate_w'], 'L1_ffn_w_gate': _L1_ffn_in['w_gate'], 'L1_ffn_w_up': _L1_ffn_in['w_up'], 'L1_ffn_w_down': _L1_ffn_in['w_down'], 'L1_ffn_sh_gate': _L1_ffn_in['sh_gate'], 'L1_ffn_sh_up': _L1_ffn_in['sh_up'], 'L1_ffn_sh_down': _L1_ffn_in['sh_down']}
    _x0 = _d['L0_attn_x']
    _d['L0_attn_x'] = jax.random.normal(jax.random.fold_in(jax.random.key(seed), 1), (4, 512, 256), dtype=_x0.dtype)
    del _x0
    return _d

def reference(L0_attn_x, L0_attn_Wq, L0_attn_bq, L0_attn_Wkv, L0_attn_bkv, L0_ffn_gate_w, L0_ffn_w_gate, L0_ffn_w_up, L0_ffn_w_down, L1_attn_W_xproj, L1_attn_W_dt, L1_attn_b_dt, L1_attn_A_log, L1_attn_D_param, L1_ffn_gate_w, L1_ffn_w_gate, L1_ffn_w_up, L1_ffn_w_down, L1_ffn_sh_gate, L1_ffn_sh_up, L1_ffn_sh_down):

    def _L0_attn_ref(x, Wq, bq, Wkv, bkv):
        import jax, jax.numpy as jnp
        import numpy as np
        import math
        B, L, E, H = (4, 512, 256, 16)
        HD = E // H
        b, l, e = x.shape
        hd = Wkv.shape[0] // 2
        h = e // hd
        q = (x @ Wq.T + bq).reshape(b, l, h, hd)
        kv = (x @ Wkv.T + bkv).reshape(b, l, 2, hd)
        k, v = (kv[:, :, 0], kv[:, :, 1])
        attn = jnp.einsum('blhd,bld->blh', q, k)[..., None] / math.sqrt(hd)
        attn = jax.nn.softmax(attn, axis=-1)
        out = (attn * v[:, :, None, :]).reshape(b, l, -1)
        return out

    def _L0_ffn_ref(hidden_states, gate_w, w_gate, w_up, w_down):
        import jax, jax.numpy as jnp
        import numpy as np
        B, S, D, FF, E = (4, 256, 256, 1024, 2)
        b, s, d = hidden_states.shape
        x = hidden_states.reshape(-1, d)
        logits = x @ gate_w.T
        probs = jax.nn.softmax(logits.astype(jnp.float32), axis=-1)
        sel = jnp.argmax(probs, axis=-1)
        top_w = jnp.take_along_axis(probs, sel[:, None], axis=-1)
        onehot = jax.nn.one_hot(sel, gate_w.shape[0], dtype=x.dtype)
        g = jnp.einsum('td,efd->etf', x, w_gate)
        u = jnp.einsum('td,efd->etf', x, w_up)
        h = jax.nn.silu(g) * u
        y = jnp.einsum('etf,edf->etd', h, w_down)
        out = jnp.einsum('etd,te->td', y, onehot * top_w)
        return out.reshape(b, s, d)

    def _L1_attn_ref(x, W_xproj, W_dt, b_dt, A_log, D_param):
        import jax, jax.numpy as jnp
        import numpy as np
        BSZ, L, D_INNER, D_STATE = (2, 256, 256, 8)
        DT_RANK = D_INNER // 8
        d_state = A_log.shape[1]
        dt_rank = W_dt.shape[1]
        x_dbl = jnp.einsum('bld,kd->blk', x, W_xproj)
        dt_r = x_dbl[..., :dt_rank]
        B_ssm = x_dbl[..., dt_rank:dt_rank + d_state]
        C_ssm = x_dbl[..., dt_rank + d_state:]
        delta = jax.nn.softplus(jnp.einsum('blr,dr->bld', dt_r, W_dt) + b_dt)
        A = -jnp.exp(A_log)
        dA = jnp.exp(delta[..., None] * A)
        dBu = (delta * x)[..., None] * B_ssm[:, :, None, :]

        def combine(c1, c2):
            a1, b1 = c1
            a2, b2 = c2
            return (a1 * a2, a2 * b1 + b2)
        _, h = jax.lax.associative_scan(combine, (dA, dBu), axis=1)
        y = jnp.einsum('bldn,bln->bld', h, C_ssm) + x * D_param
        return y

    def _L1_ffn_ref(hidden_states, gate_w, w_gate, w_up, w_down, sh_gate, sh_up, sh_down):
        import jax, jax.numpy as jnp
        import numpy as np
        H = 256
        F = 176
        E = 64
        TOP_K = 6
        CAP = 64
        SCALE = 1.0
        F_SH = 2 * F
        B, S = (1, 256)
        b, s, _ = hidden_states.shape
        x = hidden_states.reshape(-1, H)
        T = x.shape[0]
        logits = x.astype(jnp.float32) @ gate_w.astype(jnp.float32).T
        scores = jax.nn.softmax(logits, axis=-1)
        topk_w, topk_idx = jax.lax.top_k(scores, TOP_K)
        topk_w = topk_w * SCALE
        eid = topk_idx.reshape(-1)
        x_exp = jnp.repeat(x, TOP_K, axis=0)
        order = jnp.argsort(eid)
        eid_s = eid[order]
        counts = jnp.bincount(eid, length=E)
        starts = jnp.cumsum(counts) - counts
        pos = jnp.arange(T * TOP_K) - starts[eid_s]
        valid = pos < CAP
        pos_c = jnp.where(valid, pos, CAP)
        buf = jnp.zeros((E, CAP + 1, H), x.dtype).at[eid_s, pos_c].set(x_exp[order])
        g = jax.nn.silu(jnp.einsum('ech,ehf->ecf', buf, w_gate))
        u = jnp.einsum('ech,ehf->ecf', buf, w_up)
        d = jnp.einsum('ecf,efh->ech', g * u, w_down)
        out_s = jnp.where(valid[:, None], d[eid_s, pos_c], 0.0)
        out_exp = jnp.zeros_like(out_s).at[order].set(out_s)
        y = jnp.einsum('tkh,tk->th', out_exp.reshape(T, TOP_K, H), topk_w)
        y = y.astype(x.dtype).reshape(b, s, H)
        gs = jax.nn.silu(hidden_states @ sh_gate.T)
        us = hidden_states @ sh_up.T
        y = y + gs * us @ sh_down.T
        return y
    x = L0_attn_x
    x = x + _L0_attn_ref(_layernorm(x, axis=-1), L0_attn_Wq, L0_attn_bq, L0_attn_Wkv, L0_attn_bkv)
    x = x + _L0_ffn_ref(_layernorm(x, axis=-1), L0_ffn_gate_w, L0_ffn_w_gate, L0_ffn_w_up, L0_ffn_w_down)
    x = x + _L1_attn_ref(_layernorm(x, axis=-1), L1_attn_W_xproj, L1_attn_W_dt, L1_attn_b_dt, L1_attn_A_log, L1_attn_D_param)
    x = x + _L1_ffn_ref(_layernorm(x, axis=-1), L1_ffn_gate_w, L1_ffn_w_gate, L1_ffn_w_up, L1_ffn_w_down, L1_ffn_sh_gate, L1_ffn_sh_up, L1_ffn_sh_down)
    return x

_drawn_inputs = setup_inputs


def setup_inputs(seed=0):
    import zlib

    import numpy as np

    out = dict(_drawn_inputs(seed))
    spreads = {'L1_attn_D_param': (1.0, 0.2)}
    factors = {'L0_ffn_gate_w': 5.118,
     'L0_ffn_w_gate': 3.97,
     'L0_ffn_w_up': 3.919,
     'L0_ffn_w_down': 3.922,
     'L1_attn_W_xproj': 5.682,
     'L1_attn_W_dt': 8.0,
     'L1_attn_b_dt': 8.0,
     'L1_attn_A_log': 8.0,
     'L1_ffn_gate_w': 8.0,
     'L1_ffn_w_gate': 8.0,
     'L1_ffn_w_up': 8.0,
     'L1_ffn_w_down': 8.0,
     'L1_ffn_sh_gate': 7.007,
     'L1_ffn_sh_up': 6.907,
     'L1_ffn_sh_down': 6.898}
    for name, (base, spread) in spreads.items():
        noise = np.random.default_rng([zlib.crc32(name.encode()), seed]).standard_normal(out[name].shape)
        drawn = base * np.exp(spread * noise) if base else spread * noise
        out[name] = jnp.asarray(drawn.astype(out[name].dtype))
    for name, factor in factors.items():
        out[name] = (out[name] * factor).astype(out[name].dtype)
    return out
```

```python
from contextlib import ExitStack

import concourse.bass as bass
from concourse import mybir

F32 = mybir.dt.float32
U32 = mybir.dt.uint32
I32 = mybir.dt.int32
ALU = mybir.AluOpType
ACT = mybir.ActivationFunctionType
AX = mybir.AxisListType.X

P = 128
B, L, D = 4, 512, 256
N = B * L
J = L // P
K = D // P
H, HD = 16, 16
QKV = D + 2 * HD
FF = 1024
HALF = FF // 512
S0 = J + 1
SLOTS = S0 * P
STEPS = S0 * HALF
NS = 8
R = D // 8
GROUP = 2
GROUPS = K * NS // GROUP
E, CAP, TOPK, F1 = 64, 64, 6, 176
FC = F1 // 2
PAIRS = E // 2
RING = 4
ROW_RING = 8
FSH = 2 * F1
SH_ROWS = [128, 128, FSH - 256]
XW = D + E
ROWS = N + CAP
EPS = 1e-5
HALF_EXPONENT = 0x5F3759DF
NEWTON = 3
LN = 3 * J + 3 + 3 * NEWTON
AT_DIFF, AT = 4, 9
RT_SEL, RT_DIFF, RT = 10, 11, 22
LOG1P = [0.999999995, -0.49999904, 0.33330004, -0.249545589, 0.196781173, -0.153118631, 0.106142647,
         -0.0570642008, 0.019907161, -0.00325637848]
ZS = len(LOG1P) + 1
GT = 4
TOP = 2 * J + 3
ROUNDS = CAP // 8
RD = 2 * ROUNDS + 1


class Ring:

    def __init__(self, slots, uses_before, uses_pipelined):
        self.slots, self.before, self.per = slots, uses_before, uses_pipelined
        self.k, self.shift = 0, 0
        self.wide = True

    def enter(self, turn):
        self.wide = True
        if turn is None:
            self.k, self.shift = 0, 0
        else:
            self.k, self.shift = self.before, turn * self.per

    def next(self, uses=1):
        k = self.k
        self.free_at = self.shift + k - (0 if self.wide else 1)
        self.wide = uses > 1
        self.k += uses
        return k % self.slots, self.shift + k

    def so_far(self):
        return self.shift + self.k


def wait_from_one(eng, sem, value):
    if not isinstance(value, int) or value > 0:
        eng.wait_ge(sem, value)


def wait_apart(eng, passed, *waits):
    for sem, value in waits:
        wait_from_one(eng, sem, value)
    if any(not isinstance(v, int) for _, v in waits):
        eng.sem_inc(passed, 1)


def build(nc, x, wq_t, bq, wkv_t, bkv, gate0, wg0_t, wu0_t, wd0_t, wx_t, wdt_t, b_dt, a_log, d_par,
          gate1_t, wg1, wu1, wd1, shg_t, shu_t, shd_t, out):
    with ExitStack() as ctx:
        def sb(name, shape, dt=F32):
            return ctx.enter_context(nc.sbuf_tensor(name, shape, dt))

        def ps(name):
            return ctx.enter_context(nc.psum_tensor(name, [P, 512], F32))

        def sem(name):
            return ctx.enter_context(nc.semaphore(name))

        x_res = sb("x_res", [P, B * J, D])
        ident = sb("ident", [P, P])
        before_me = sb("before_me", [P, P])
        ones = sb("ones", [P, P])
        tok_local = sb("tok_local", [P, J])
        last_slot = sb("last_slot", [P, J])
        tok_value = sb("tok_value", [P, B * J])
        tile_thr = sb("tile_thr", [1, S0])
        place_no = sb("place_no", [CAP, CAP])

        w_qkv = sb("w_qkv", [P, K, QKV])
        b_qkv = sb("b_qkv", [P, QKV])
        g0_row = sb("g0_row", [P, 2, D])
        big = sb("big", [P, 2 * K * 2 * FF + 2 * 8 * D])
        gu0 = big[:, 0:2 * K * 2 * FF].rearrange("p (e k g f) -> p e k g f", e=2, k=K, g=2)
        dn0 = big[:, 2 * K * 2 * FF:].rearrange("p (e c d) -> p e c d", e=2, c=8)
        gu1 = [big[:, s * 4 * FSH:(s + 1) * 4 * FSH].rearrange("p (a f) -> p a f", a=4) for s in range(RING)]
        dn1 = [big[0:FC, RING * 4 * FSH + s * 4 * D:RING * 4 * FSH + (s + 1) * 4 * D]
               .rearrange("p (a d) -> p a d", a=4) for s in range(RING)]
        w_x = sb("w_x", [P, K, R + 2 * NS])
        w_dt = sb("w_dt", [R, D])
        bdt_col = sb("bdt_col", [P, K])
        a_col = sb("a_col", [P, K, NS])
        d_row = sb("d_row", [P, D])
        w_g1 = sb("w_g1", [P, K, E])
        w_sh = sb("w_sh", [P, K, 2, FSH])
        w_shd = sb("w_shd", [P, 3, D])

        ln_st = [sb(f"ln_st{i}", [P, J, 6]) for i in range(4)]
        ln_mv = [sb(f"ln_mv{i}", [P, J, 2]) for i in range(4)]
        ln_w = [sb(f"ln_w{i}", [P, 3, J]) for i in range(4)]

        xn_f = sb("xn_f", [P, J, D])
        front_t = sb("front_t", [P, K * S0 * P])
        xn_attn_t = front_t[:, 0:K * J * P].rearrange("p (k j t) -> p k j t", k=K, j=J)
        xs_t = front_t[:].rearrange("p (k j t) -> p k j t", k=K, j=S0)
        act_buf = sb("act_buf", [P, 4 * 512])
        h0 = act_buf[:, 0:1024].rearrange("p (s f) -> p s f", s=2)
        h0_t = act_buf[:, 1024:2048].rearrange("p (s f) -> p s f", s=2)
        qkv = act_buf[:, 0:J * QKV].rearrange("p (j n) -> p j n", j=J)
        att_s = sb("att_s", [P, 7, J * H])
        mix = sb("mix", [P, J, D])
        rt = sb("rt", [P, 13, 2 * J])
        rt_ex = sb("rt_ex", [1, S0], I32)
        slot_idx = sb("slot_idx", [P, J], U32)
        xs = sb("xs", [P, S0, D])
        sig = sb("sig", [P, 2, 512])

        xf = sb("xf", [P, J, XW])
        back_t = sb("back_t", [P, K, J, P])
        y_fm = back_t[:].rearrange("p k j t -> p k (j t)")
        x_dbl = sb("x_dbl", [R + 2 * NS, L])
        bc = sb("bc", [P, 2 * NS, L])
        sp_z = sb("sp_z", [P, K, L])
        hsh_t = sb("hsh_t", [P, 3, L])
        sp_e = hsh_t[:, 0:K, :]
        io_buf = sb("io_buf", [P, J * D])
        y_tok = io_buf[:].rearrange("p (j d) -> p j d", j=J)
        o_sb = y_tok
        delta = sb("delta", [P, K, L])
        d_a = sb("d_a", [P, 2, GROUP, L])
        hs = sb("hs", [P, 2, GROUP, L])
        y_half = sb("y_half", [P, L])
        sc = sb("sc", [P, J, E])
        sc66 = sb("sc66", [P, J, E + 2])
        sc_s = sb("sc_s", [P, 3, J])
        top = sb("top", [P, J, 8])
        marked = sb("marked", [P, J, E + 2])
        work = sb("work", [CAP, CAP + L])
        keep = sb("keep", [CAP, CAP])

        ids = sb("ids", [CAP, 2, CAP])
        ids_z = sb("ids_z", [CAP, CAP])
        idx_get = sb("idx_get", [P, PAIRS], U32)
        idx_add = sb("idx_add", [CAP, E], U32)
        area = bc[:].rearrange("p n l -> p (n l)")
        at = [0]

        def carve(n):
            at[0] += n
            return area[:, at[0] - n:at[0]]

        ids_t = carve(E)
        xg = [carve(XW) for _ in range(ROW_RING)]
        xg_t = carve(2 * K * P).rearrange("p (s k t) -> p s k t", s=2, k=K)
        sig1 = carve(2 * F1).rearrange("p (s f) -> p s f", s=2)
        h1 = carve(2 * F1).rearrange("p (s f) -> p s f", s=2)
        h1_t = carve(4 * P)[0:FC, :].rearrange("p (s c t) -> p s c t", s=2, c=2)
        yo = carve(2 * D).rearrange("p (s d) -> p s d", s=2)
        clear = carve(XW)

        gate_ps = [ps("gate_ps0"), ps("gate_ps1")]
        up_ps = [ps("up_ps0"), ps("up_ps1")]
        turn_ps = [ps("turn_ps0"), ps("turn_ps1")]
        down_ps = ps("down_ps")
        misc_ps = ps("misc_ps")

        y_ps = [down_ps, misc_ps]

        sorted_dram = nc.dram_tensor("sorted_dram", (SLOTS, D), F32).ap()
        ysorted_dram = nc.dram_tensor("ysorted_dram", (SLOTS, D), F32).ap()
        bc_dram = nc.dram_tensor("bc_dram", (2 * NS, L), F32).ap()
        table = nc.dram_tensor("table", (ROWS, XW), F32).ap()
        odd_out = nc.dram_tensor("odd_out", (ROWS, D), F32).ap()

        x_loaded = [sem(f"x_loaded{b}") for b in range(B)]
        w_attn_loaded = sem("w_attn_loaded")
        w_ffn_loaded = sem("w_ffn_loaded")
        w_ssm_loaded = sem("w_ssm_loaded")
        w_tail_loaded = sem("w_tail_loaded")
        pool_consts = sem("pool_consts")
        dve_consts = sem("dve_consts")
        a_ready = sem("a_ready")
        scratch_clear = sem("scratch_clear")
        turn_filled = sem("turn_filled")
        turn_moved = sem("turn_moved")
        misc_filled = sem("misc_filled")
        misc_moved = sem("misc_moved")
        gu_filled = sem("gu_filled")
        gu_used = sem("gu_used")
        down_filled = sem("down_filled")
        down_moved = sem("down_moved")
        tanh_ready = sem("tanh_ready")
        silu_steps = sem("silu_steps")
        ln_steps = [sem(f"ln_steps{i}") for i in range(4)]
        attn_steps = sem("attn_steps")
        attn_exp = sem("attn_exp")
        route_steps = sem("route_steps")
        route_exp = sem("route_exp")
        rows_sorted = sem("rows_sorted")
        sorted_loaded = sem("sorted_loaded")
        ys_stored = sem("ys_stored")
        yt_loaded = sem("yt_loaded")
        x_after_ffn = sem("x_after_ffn")
        bc_stored = sem("bc_stored")
        bc_loaded = sem("bc_loaded")
        z_ready = sem("z_ready")
        z_steps = sem("z_steps")
        sp_funcs = sem("sp_funcs")
        du_ready = sem("du_ready")
        skip_steps = sem("skip_steps")
        da_ready = sem("da_ready")
        dbu_ready = sem("dbu_ready")
        scanned = sem("scanned")
        hc_ready = sem("hc_ready")
        sum_steps = sem("sum_steps")
        group_summed = sem("group_summed")
        x_after_ssm = sem("x_after_ssm")
        gate_steps = sem("gate_steps")
        gate_exp = sem("gate_exp")
        scores_copied = sem("scores_copied")
        top_steps = sem("top_steps")
        round_steps = sem("round_steps")
        table_stored = sem("table_stored")
        out_stored = sem("out_stored")
        ids_steps = sem("ids_steps")
        pair_loaded = [sem(f"pair_loaded{i}") for i in range(RING)]
        xg_loaded = [sem(f"xg_loaded{i}") for i in range(ROW_RING)]
        xg_turned = sem("xg_turned")
        xgt_ready = sem("xgt_ready")
        gu1_filled = sem("gu1_filled")
        tanh1_ready = sem("tanh1_ready")
        silu1_steps = sem("silu1_steps")
        h1_ready = sem("h1_ready")
        h1_turned = sem("h1_turned")
        h1t_ready = sem("h1t_ready")
        down1_filled = sem("down1_filled")
        yo_halves = sem("yo_halves")
        rows_added = [sem("even_rows_added"), sem("odd_rows_added")]
        sums_added = sem("sums_added")

        passed = {e: sem(f"passed_{e}") for e in ("sp", "pool", "pe", "dve")}

        front = [("attn_in", 0), ("attn_qkv", 0), ("attn_score", 0), ("attn_add", 0),
                 ("route_gate", 0), ("route_slots", 0), ("ffn_in", 0)] + [("ffn", s) for s in range(STEPS)] \
            + [("ffn_tail", 0), ("ffn_out", 0)]
        scan = [("ssm", 0), ("ssm", 1), ("ssm_delta", 1)] + [("ssm", g) for g in range(2, GROUPS)]
        tail = [("ssm_skip", 0), ("ssm_out", 0), ("gates_in", 0), ("gates", 0), ("places", 0)] \
            + [("shared", m) for m in range(3)] + [("shared_out", 0)]
        back = [("ssm_in", 0), ("ssm_proj", 0), ("ssm_exp", 0), ("ssm_delta", 0)] + scan + tail
        beside = {
            "ssm_in": ["attn_in"], "ssm_proj": ["attn_qkv"], "ssm_exp": ["attn_score"],
            "ssm_delta0": ["attn_add", "route_gate"], "ssm0": ["route_slots"], "ssm3": ["ffn_in", "ffn0"],
            "ssm5": ["ffn1"], "ssm7": ["ffn2"], "ssm_out": ["ffn3"], "gates_in": ["ffn4"], "gates": ["ffn5"],
            "places": ["ffn6"], "shared0": ["ffn7"], "shared1": ["ffn8"], "shared2": ["ffn9", "ffn_tail"],
            "shared_out": ["ffn_out"]}
        by_key = {name + (str(s) if name == "ffn" else ""): (name, s) for name, s in front}
        both = []
        for name, s in back:
            both.append(("B", name, s))
            for key in beside.get(name, beside.get(name + str(s), [])):
                both.append(("F", *by_key[key]))
        TURNS = dict(attn_in=2, ffn_in=3, ffn=1, ffn_tail=1, ssm_in=2, ssm_out=2, gates_in=2, places=1)
        MISCS = dict(attn_qkv=J, route_slots=1, ssm_proj=1 + K, gates=1, shared_out=2)
        T_F, T_B = 2 + 3 + STEPS, 2 + 2 + 2 + 1
        M_F, M_B = J + 1, 1 + K + 1 + 2
        G_F, G_B = STEPS, 4

        def rings():
            return (Ring(2, T_F, T_F + T_B), Ring(1, M_F, M_F + M_B), Ring(2, G_F, G_F + G_B),
                    Ring(1, STEPS, STEPS + 3))

        def run(eng, stages, ring_set, skips=()):
            def stage(name, b, s):
                for ring, uses, mine in skips:
                    if name in uses and name not in mine and not (name == "ffn" and s == 0):
                        ring.next(uses[name])
                if name in stages:
                    stages[name](b, s)

            for r in ring_set:
                r.enter(None)
            for name, s in front:
                stage(name, 0, s)
            with eng.Fori(0, B - 1) as i:
                for r in ring_set:
                    r.enter(i)
                for side, name, s in both:
                    stage(name, i + 1 if side == "F" else i, s)
            for r in ring_set:
                r.enter(B - 1)
            for name, s in back:
                stage(name, B - 1, s)

        def run_pairs(eng, part):
            last = PAIRS // ROW_RING - 1
            for q in range(ROW_RING):
                part(q, q, 0)
            with eng.Fori(1, last) as i:
                for q in range(ROW_RING):
                    part(i * ROW_RING + q, q, i)
            for q in range(ROW_RING):
                part(ROW_RING * last + q, q, last)

        block = ctx.enter_context(nc.Block())

        @block.sync
        def _(sp):
            _, misc, _, _ = rings()

            def row(v, n):
                return v.rearrange("(o n) -> o n", o=1).broadcast_to([P, n])

            xv = x.rearrange("(t p) d -> p t d", p=P)
            sp.dma_start(x_res[:, 0:J, :], xv[:, 0:J, :]).then_inc(x_loaded[0], 16)
            sp.dma_start(w_qkv[:, :, 0:D], wq_t.rearrange("(k p) n -> p k n", p=P)).then_inc(w_attn_loaded, 16)
            sp.dma_start(w_qkv[:, :, D:QKV], wkv_t.rearrange("(k p) n -> p k n", p=P)).then_inc(w_attn_loaded, 16)
            sp.dma_start(b_qkv[:, 0:D], row(bq, D)).then_inc(w_attn_loaded, 16)
            sp.dma_start(b_qkv[:, D:QKV], row(bkv, 2 * HD)).then_inc(w_attn_loaded, 16)
            sp.dma_start(g0_row[:].rearrange("p e d -> p (e d)"),
                         row(gate0.rearrange("e d -> (e d)"), 2 * D)).then_inc(w_attn_loaded, 16)
            for e in range(2):
                for g, w in ((0, wg0_t), (1, wu0_t)):
                    sp.dma_start(gu0[:, e, :, g, :], w[e].rearrange("(k p) f -> p k f", p=P)
                                 ).then_inc(w_ffn_loaded, 16)
                sp.dma_start(dn0[:, e, :, :], wd0_t[e].rearrange("(c p) d -> p c d", p=P)).then_inc(w_ffn_loaded, 16)
            for b in range(1, B):
                sp.dma_start(x_res[:, b * J:(b + 1) * J, :], xv[:, b * J:(b + 1) * J, :]).then_inc(x_loaded[b], 16)
            sp.dma_start(a_col[:], a_log.rearrange("(k p) n -> p k n", p=P)).then_inc(w_ssm_loaded, 16)
            sp.dma_start(w_x[:], wx_t.rearrange("(k p) n -> p k n", p=P)).then_inc(w_ssm_loaded, 16)
            sp.dma_start(w_dt[:], wdt_t).then_inc(w_ssm_loaded, 16)
            sp.dma_start(bdt_col[:], b_dt).then_inc(w_ssm_loaded, 16)
            sp.dma_start(d_row[:], row(d_par, D)).then_inc(w_ssm_loaded, 16)
            sp.dma_start(w_g1[:], gate1_t.rearrange("(k p) n -> p k n", p=P)).then_inc(w_tail_loaded, 16)
            for g, w in ((0, shg_t), (1, shu_t)):
                sp.dma_start(w_sh[:, :, g, :], w.rearrange("(k p) f -> p k f", p=P)).then_inc(w_tail_loaded, 16)
            sp.dma_start(w_shd[:, 0:2, :], shd_t[0:256, :].rearrange("(c p) d -> p c d", p=P)).then_inc(w_tail_loaded, 16)
            sp.dma_start(w_shd[0:SH_ROWS[2], 2, :], shd_t[256:FSH, :]).then_inc(w_tail_loaded, 16)

            def ffn_in(b, _):
                wait_apart(sp, passed["sp"], (rows_sorted, (b + 1) * 16 * J))
                wait_apart(sp, passed["sp"], (ys_stored, b * 16))
                sp.dma_start(xs[:], sorted_dram.rearrange("(s p) d -> p s d", p=P)).then_inc(sorted_loaded, 16)

            def ffn_out(b, _):
                wait_apart(sp, passed["sp"], (down_moved, (b + 1) * S0))
                wait_apart(sp, passed["sp"], (yt_loaded, b * 16 * J))
                sp.dma_start(ysorted_dram.rearrange("(s p) d -> p s d", p=P), xs[:]).then_inc(ys_stored, 16)

            def ssm_proj(b, _):
                _, use = misc.next(1 + K)
                wait_apart(sp, passed["sp"], (misc_moved, use + 1))
                sp.dma_start(bc_dram, x_dbl[R:R + 2 * NS, :]).then_inc(bc_stored, 16)
                wait_apart(sp, passed["sp"], (bc_stored, (b + 1) * 16))
                wait_apart(sp, passed["sp"], (hc_ready, b * GROUPS))
                sp.dma_start(bc[:].rearrange("p n l -> p (n l)"),
                             bc_dram.rearrange("(o n) l -> o (n l)", o=1).broadcast_to([P, 2 * NS * L])
                             ).then_inc(bc_loaded, 16)

            def places(b, _):
                wait_apart(sp, passed["sp"], (scores_copied, b + 1))
                sp.dma_start(table[0:N, :].rearrange("(b j p) d -> p b j d", b=B, p=P)[:, b, :, :],
                             xf[:]).then_inc(table_stored, 16)

            def shared_out(b, _):
                _, use = misc.next(2)
                wait_apart(sp, passed["sp"], (misc_moved, use + 2))
                sp.dma_start(out[0:N, :].rearrange("(b j p) d -> p b j d", b=B, p=P)[:, b, :, :],
                             o_sb).then_inc(out_stored, 16)

            sp.wait_ge(scratch_clear, 64)
            run(sp, dict(ffn_in=ffn_in, ffn_out=ffn_out, ssm_proj=ssm_proj, places=places, shared_out=shared_out), [misc],
                [(misc, MISCS, ("ssm_proj", "shared_out"))])

            def weights(p, q, i):
                if isinstance(p, int) and p < RING:
                    sp.wait_ge(down_filled, B * S0)
                else:
                    wait_apart(sp, passed["sp"], (down1_filled, p - RING + 1))
                for g, w in ((0, wg1), (1, wu1)):
                    sp.dma_start(gu1[q % RING][:, :, g * F1:(g + 1) * F1],
                                 w.rearrange("(n e) (k p) f -> p n (e k) f", e=2, p=P)[:, p, :, :]
                                 ).then_inc(pair_loaded[q % RING], 16)
                sp.dma_start(dn1[q % RING], wd1.rearrange("(n e) (c p) d -> p n (e c) d", e=2, p=FC)[:, p, :, :]
                             ).then_inc(pair_loaded[q % RING], 16)

            run_pairs(sp, weights)
            sp.wait_ge(out_stored, 16 * B)
            for added in rows_added:
                sp.wait_ge(added, 16 * PAIRS)
            sp.wait_ge(sums_added, 16)

        @block.gpsimd
        def _(pool):
            tt = nc.gpsimd.tensor_tensor

            nc.gpsimd.memset(clear, 0.0).then_inc(pool_consts, 1)
            nc.gpsimd.memset(ones[:], 1.0).then_inc(pool_consts, 1)
            nc.gpsimd.memset(ident[:], 0.0).then_inc(pool_consts, 1)
            pool.wait_ge(pool_consts, 3)
            nc.gpsimd.affine_select(out=ident[:], in_=ident[:], compare_op=ALU.not_equal, fill=1.0, base=0,
                                    pattern=[[-1, P]], channel_multiplier=1).then_inc(pool_consts, 1)
            nc.gpsimd.affine_select(out=before_me[:], in_=ones[:], compare_op=ALU.is_gt, fill=0.0, base=0,
                                    pattern=[[1, P]], channel_multiplier=-1).then_inc(pool_consts, 1)
            for dst, pattern, base, mult in ((tok_local[:], [[P, J]], 0, 1),
                                             (last_slot[:], [[-P, J]], SLOTS - 1, -1),
                                             (tok_value[:], [[-P, B * J]], N, -1),
                                             (tile_thr[:], [[-P, S0]], L, 0),
                                             (place_no[:], [[1, CAP]], 0, 0)):
                nc.gpsimd.iota(dst, pattern, base=base, channel_multiplier=mult,
                               allow_small_or_imprecise_dtypes=True).then_inc(pool_consts, 1)
            pool.dma_start(sorted_dram.rearrange("(s p) d -> p s d", p=P),
                           clear[:, 0:D].unsqueeze(1).broadcast_to([P, S0, D])).then_inc(scratch_clear, 16)
            pool.dma_start(table[N:ROWS, :], clear[0:CAP, :]).then_inc(scratch_clear, 16)
            pool.dma_start(out[N:ROWS, :], clear[0:CAP, 0:D]).then_inc(scratch_clear, 16)
            pool.dma_start(odd_out.rearrange("(a p) d -> p a d", p=CAP),
                           clear[0:CAP, 0:D].unsqueeze(1).broadcast_to([CAP, ROWS // CAP, D])
                           ).then_inc(scratch_clear, 16)
            pool.wait_ge(scratch_clear, 64)

            def route_slots(b, _):
                wait_apart(pool, passed["pool"], (ln_steps[1], (b + 1) * LN), (route_steps, (b + 1) * RT),
                           (sorted_loaded, b * 16))
                for j in range(J):
                    pool.indirect_dma_start(sorted_dram, bass.IndirectOffsetOnAxis(slot_idx[:, j:j + 1], 0),
                                            xn_f[:, j, :], None).then_inc(rows_sorted, 16)

            def ffn_out(b, _):
                wait_apart(pool, passed["pool"], (ys_stored, (b + 1) * 16))
                for j in range(J):
                    pool.indirect_dma_start(mix[:, j, :], None, ysorted_dram,
                                            bass.IndirectOffsetOnAxis(slot_idx[:, j:j + 1], 0)).then_inc(yt_loaded, 16)

            def ssm_delta(b, c):
                pool.wait_ge(z_steps, (b * K + c + 1) * ZS)
                tt(sp_z[:, c, :], delta[:, c, :], y_fm[:, c, :], ALU.mult).then_inc(du_ready, 1)
                if c == 0:
                    pool.wait_ge(bc_loaded, (b + 1) * 16)
                    delta_b(b, 0)

            def ssm_skip(b, _):
                xn = xf[:, :, 0:D]
                tt(xn, xn, d_row[:].unsqueeze(1).broadcast_to([P, J, D]), ALU.mult).then_inc(skip_steps, 1)
                pool.wait_ge(skip_steps, b * 2 + 1)
                xb = x_res[:, bass.ds(b * J, J), :]
                tt(xb, xb, xn, ALU.add).then_inc(skip_steps, 1)

            def delta_b(b, g):
                c, n0 = g // (NS // GROUP), g % (NS // GROUP) * GROUP
                wait_from_one(pool, group_summed, b * GROUPS + max(g - 1, 0))
                pool.wait_ge(du_ready, b * K + c + 1)
                tt(hs[:, g % 2, :, :], sp_z[:, c, :].unsqueeze(1).broadcast_to([P, GROUP, L]), bc[:, n0:n0 + GROUP, :],
                   ALU.mult).then_inc(dbu_ready, 1)

            def ssm(b, g):
                if g + 1 < GROUPS:
                    delta_b(b, g + 1)

            def gates(b, _):
                wait_apart(pool, passed["pool"], (gate_steps, (b + 1) * GT))
                nc.gpsimd.tensor_copy(xf[:, :, D:XW], sc66[:, :, 0:E]).then_inc(scores_copied, 1)

            run(pool, dict(route_slots=route_slots, ffn_out=ffn_out, ssm_delta=ssm_delta, ssm=ssm, ssm_skip=ssm_skip, gates=gates), [])

            def fetch(p):
                pool.indirect_dma_start(xg[p % ROW_RING], None, table,
                                        bass.IndirectOffsetOnAxis(idx_get[:, p:p + 1], 0)
                                        ).then_inc(xg_loaded[p % ROW_RING], 16)

            pool.wait_ge(ids_steps, 6)
            pool.wait_ge(table_stored, 16 * B)
            pool.wait_ge(out_stored, 16 * B)
            for p in range(ROW_RING):
                fetch(p)
            for p in range(PAIRS):
                pool.wait_ge(yo_halves, 2 * (p + 1))
                for e in range(2):
                    wait_from_one(pool, rows_added[e], 16 * p)
                    pool.indirect_dma_start((out, odd_out)[e],
                                            bass.IndirectOffsetOnAxis(idx_add[:, 2 * p + e:2 * p + e + 1], 0),
                                            yo[e * CAP:(e + 1) * CAP, p % 2, :], None, compute_op=ALU.add
                                            ).then_inc(rows_added[e], 16)
                if p + ROW_RING < PAIRS:
                    fetch(p + ROW_RING)
            pool.wait_ge(rows_added[0], 16 * PAIRS)
            pool.wait_ge(rows_added[1], 16 * PAIRS)
            pool.dma_start(out[0:N, :].rearrange("(p r) d -> p (r d)", p=P),
                           odd_out[0:N, :].rearrange("(p r) d -> p (r d)", p=P), accum_op=ALU.add, max_dma_last_dim=8192
                           ).then_inc(sums_added, 16)

        @block.tensor
        def _(pe):
            turn, misc, gu, _ = rings()
            expert_of, gu_use, h_use = {}, {}, {}

            def transposes(blocks, *ready):
                slot, use = turn.next()
                wait_apart(pe, passed["pe"], (turn_moved, use - 1), *ready)
                for col, rows, width, src in blocks:
                    mm = pe.transpose(turn_ps[slot][0:width, col:col + rows], src, ident[0:rows, 0:rows])
                mm.then_inc(turn_filled, 1)

            def turn_tiles(src, tiles):
                for j0 in range(0, tiles, 2):
                    transposes([((jj * K + k) * P, P, P, src[:, j0 + jj, k * P:(k + 1) * P])
                                for jj in range(min(2, tiles - j0)) for k in range(K)])
                pe.wait_ge(turn_moved, turn.so_far())

            def attn_in(b, _):
                if isinstance(b, int):
                    pe.wait_ge(pool_consts, 10)
                    pe.wait_ge(w_attn_loaded, 16 * 5)
                pe.wait_ge(ln_steps[0], (b + 1) * LN)
                turn_tiles(xn_f, J)

            def attn_qkv(b, _):
                for j in range(J):
                    _, use = misc.next()
                    wait_from_one(pe, misc_moved, use)
                    for k in range(K):
                        mm = pe.matmul(misc_ps[:, 0:QKV], xn_attn_t[:, k, j, :], w_qkv[:, k, :],
                                       start=(k == 0), stop=(k == K - 1))
                    mm.then_inc(misc_filled, 1)

            def route_slots(b, _):
                pe.wait_ge(route_steps, b * RT + RT_SEL)
                _, use = misc.next()
                wait_from_one(pe, misc_moved, use)
                pe.matmul(misc_ps[:, 0:J], before_me[:], rt[:, 6, 0:J], start=True, stop=True)
                pe.matmul(misc_ps[:, J:2 * J], ones[:], rt[:, 6, 0:J], start=True, stop=True).then_inc(misc_filled, 1)

            def ffn_in(b, _):
                if isinstance(b, int):
                    pe.wait_ge(w_ffn_loaded, 16 * 6)
                wait_apart(pe, passed["pe"], (route_steps, (b + 1) * RT))
                for j in range(S0):
                    expert_of[j] = pe.value_load(rt_ex[0:1, j:j + 1], min_val=0, max_val=1)
                pe.wait_ge(sorted_loaded, (b + 1) * 16)
                turn_tiles(xs, S0)

            def gate_up(b, s):
                j, half = s // HALF, s % HALF
                slot, use = gu.next()
                gu_use[s] = use
                wait_from_one(pe, gu_used, gu.free_at)
                for g, bank in ((0, gate_ps[slot]), (1, up_ps[slot])):
                    for k in range(K):
                        mm = pe.matmul(bank[:], xs_t[:, k, j, :],
                                       gu0[:, expert_of[j], k, g, half * 512:(half + 1) * 512],
                                       start=(k == 0), stop=(k == K - 1))
                mm.then_inc(gu_filled, 1)

            def turn_h(b, s):
                pe.wait_ge(gu_used, gu_use[s] + 1)
                h_use[s] = turn.so_far()
                transposes([(c * P, P, P, h0[:, s % 2, c * P:(c + 1) * P]) for c in range(4)])

            def down(b, s):
                j, half = s // HALF, s % HALF
                pe.wait_ge(turn_moved, h_use[s] + 1)
                if half == 0:
                    wait_from_one(pe, down_moved, b * S0 + j)
                for c in range(4):
                    mm = pe.matmul(down_ps[:, 0:D], h0_t[:, s % 2, c * P:(c + 1) * P],
                                   dn0[:, expert_of[j], half * 4 + c, :],
                                   start=(half == 0 and c == 0), stop=(half == 1 and c == 3))
                if half == 1:
                    mm.then_inc(down_filled, 1)

            def ffn(b, s):
                gate_up(b, s)
                if s >= 1:
                    turn_h(b, s - 1)
                if s >= 2:
                    down(b, s - 2)

            def ffn_tail(b, _):
                turn_h(b, STEPS - 1)
                down(b, STEPS - 2)
                down(b, STEPS - 1)

            def ssm_in(b, _):
                pe.wait_ge(w_ssm_loaded, 16 * 5)
                pe.wait_ge(ln_steps[2], (b + 1) * LN)
                turn_tiles(xf, J)

            def ssm_proj(b, _):
                _, use = misc.next()
                pe.wait_ge(misc_moved, use)
                for k in range(K):
                    mm = pe.matmul(misc_ps[0:R + 2 * NS, :], w_x[:, k, :], y_fm[:, k, :],
                                   start=(k == 0), stop=(k == K - 1))
                mm.then_inc(misc_filled, 1)
                for c in range(K):
                    _, use = misc.next()
                    pe.wait_ge(misc_moved, use)
                    pe.matmul(misc_ps[:], w_dt[:, c * P:(c + 1) * P], x_dbl[0:R, :], start=True, stop=True
                              ).then_inc(misc_filled, 1)

            def ssm_out(b, _):
                pe.wait_ge(group_summed, (b + 1) * GROUPS)
                for j0 in range(0, J, 2):
                    transposes([((jj * K + c) * P, P, P, y_fm[:, c, (j0 + jj) * P:(j0 + jj + 1) * P])
                                for jj in range(2) for c in range(K)])

            def gates_in(b, _):
                pe.wait_ge(w_tail_loaded, 16 * 5)
                pe.wait_ge(ln_steps[3], (b + 1) * LN)
                turn_tiles(xf, J)

            def gates(b, _):
                _, use = misc.next()
                pe.wait_ge(misc_moved, use)
                for j in range(J):
                    for k in range(K):
                        mm = pe.matmul(misc_ps[:, j * E:(j + 1) * E], back_t[:, k, j, :], w_g1[:, k, :],
                                       start=(k == 0), stop=(k == K - 1))
                mm.then_inc(misc_filled, 1)

            def places(b, _):
                transposes([(j * P, P, E, marked[:, j, 0:E]) for j in range(J)], (top_steps, (b + 1) * TOP))

            def shared(b, m):
                rows = SH_ROWS[m]
                slot, use = gu.next(2 if m == 2 else 1)
                pe.wait_ge(gu_used, gu.free_at)
                for g, bank in ((0, gate_ps[slot]), (1, up_ps[slot])):
                    for k in range(K):
                        mm = pe.matmul(bank[0:rows, :], w_sh[:, k, g, m * P:m * P + rows], y_fm[:, k, :],
                                       start=(k == 0), stop=(k == K - 1))
                    if g == 1 or m == 2:
                        mm.then_inc(gu_filled, 1)

            def shared_out(b, _):
                pe.wait_ge(gu_used, gu.so_far())
                for j0 in range(0, J, 2):
                    _, use = misc.next()
                    pe.wait_ge(misc_moved, use)
                    for jj in range(2):
                        for m, rows in enumerate(SH_ROWS):
                            mm = pe.matmul(misc_ps[:, jj * D:(jj + 1) * D],
                                           hsh_t[0:rows, m, (j0 + jj) * P:(j0 + jj + 1) * P],
                                           w_shd[0:rows, m, :], start=(m == 0), stop=(m == 2))
                    mm.then_inc(misc_filled, 1)

            run(pe, dict(attn_in=attn_in, attn_qkv=attn_qkv, route_slots=route_slots, ffn_in=ffn_in, ffn=ffn,
                         ffn_tail=ffn_tail, ssm_in=ssm_in, ssm_proj=ssm_proj, ssm_out=ssm_out, gates_in=gates_in,
                         gates=gates, places=places, shared=shared, shared_out=shared_out),
                [turn, misc, gu])

            pe.wait_ge(ids_steps, 3)
            transposes([(0, CAP, P, ids[:].rearrange("e a s -> e (a s)"))])
            pe.wait_ge(turn_moved, turn.so_far())

            def turn_rows(p, slot, count):
                pe.wait_ge(xg_loaded[slot], 16 * count)
                wait_from_one(pe, xgt_ready, p)
                for k in range(K):
                    mm = pe.transpose(turn_ps[0][:, k * P:(k + 1) * P], xg[slot][:, k * P:(k + 1) * P], ident[:])
                mm.then_inc(xg_turned, 1)

            def gate_up1(p, q, i):
                pe.wait_ge(pair_loaded[q % RING], 48 * (i * (ROW_RING // RING) + q // RING + 1))
                pe.wait_ge(xgt_ready, p + 1)
                wait_from_one(pe, h1_ready, p - 1)
                for k in range(K):
                    for e in range(2):
                        mm = pe.matmul(gate_ps[q % 2][e * CAP:(e + 1) * CAP, 0:FSH],
                                       xg_t[:, q % 2, k, e * CAP:(e + 1) * CAP], gu1[q % RING][:, e * K + k, :],
                                       start=(k == 0), stop=(k == K - 1))
                mm.then_inc(gu1_filled, 1)

            def turn_h1(p, par):
                pe.wait_ge(h1_ready, p + 1)
                wait_from_one(pe, h1t_ready, p)
                for c in range(2):
                    mm = pe.transpose(turn_ps[1][0:FC, c * P:(c + 1) * P], h1[:, par, c * FC:(c + 1) * FC], ident[:])
                mm.then_inc(h1_turned, 1)

            def down1(p, slot):
                par = slot % 2
                pe.wait_ge(h1t_ready, p + 1)
                wait_from_one(pe, yo_halves, 2 * (p - 1))
                for c in range(2):
                    for e in range(2):
                        mm = pe.matmul(y_ps[par][e * CAP:(e + 1) * CAP, 0:D],
                                       h1_t[:, par, c, e * CAP:(e + 1) * CAP], dn1[slot % RING][:, e * 2 + c, :],
                                       start=(c == 0), stop=(c == 1))
                mm.then_inc(down1_filled, 1)

            def pair(p, q, i):
                gate_up1(p, q, i)
                if not isinstance(p, int) or p + 1 < PAIRS:
                    turn_rows(p + 1, (q + 1) % ROW_RING, i + 1 if q + 1 < ROW_RING else i + 2)
                if not isinstance(p, int) or p >= 1:
                    turn_h1(p - 1, (q - 1) % 2)
                if not isinstance(p, int) or p >= 2:
                    down1(p - 2, (q - 2) % ROW_RING)

            turn_rows(0, 0, 1)
            run_pairs(pe, pair)
            turn_h1(PAIRS - 1, (PAIRS - 1) % 2)
            down1(PAIRS - 2, (PAIRS - 2) % ROW_RING)
            down1(PAIRS - 1, (PAIRS - 1) % ROW_RING)

        @block.scalar
        def _(act):
            act.preload_act_table_set("exp_and_others")
            turn, misc, gu, _ = rings()

            def move_turned(out_ap, of_bank):
                slot, use = turn.next()
                act.wait_ge(turn_filled, use + 1)
                nc.scalar.copy(out_ap, of_bank(turn_ps[slot])).then_inc(turn_moved, 1)

            def move_tiles(dst, tiles):
                for j0 in range(0, tiles, 2):
                    w = min(2, tiles - j0)
                    move_turned(dst[:, :, j0:j0 + w, :],
                                lambda bank: bank[:, 0:w * K * P].rearrange("p (j k t) -> p k j t", j=w, k=K))

            def attn_in(b, _):
                move_tiles(xn_attn_t, J)

            def attn_score(b, _):
                act.wait_ge(attn_steps, b * AT + AT_DIFF)
                nc.scalar.activation(att_s[:, 3, :], att_s[:, 2, :], ACT.Exp, scale=HD ** -0.5).then_inc(attn_exp, 1)

            def route_gate(b, _):
                act.wait_ge(route_steps, b * RT + RT_DIFF)
                nc.scalar.activation(rt[:, 3, :], rt[:, 2, :], ACT.Exp).then_inc(route_exp, 1)

            def ffn_in(b, _):
                move_tiles(xs_t, S0)

            def half_tanh(rows, uses):
                slot, use = gu.next(uses)
                act.wait_ge(gu_filled, use + uses)
                wait_from_one(act, gu_used, gu.free_at)
                nc.scalar.activation(sig[0:rows, slot, :], gate_ps[slot][0:rows, :], ACT.Tanh, scale=0.5
                                     ).then_inc(tanh_ready, 1)

            def move_h(s):
                move_turned(h0_t[:, s % 2, :], lambda bank: bank[:])

            def move_y(b, j):
                act.wait_ge(down_filled, b * S0 + j + 1)
                nc.scalar.copy(xs[:, j, :], down_ps[:, 0:D]).then_inc(down_moved, 1)

            def ffn(b, s):
                half_tanh(P, 1)
                if s >= 1:
                    move_h(s - 1)
                if s >= 3 and (s - 2) % HALF == 1:
                    move_y(b, (s - 2) // HALF)

            def ffn_tail(b, _):
                move_h(STEPS - 1)
                move_y(b, S0 - 1)

            def ssm_in(b, _):
                move_tiles(back_t, J)

            def ssm_proj(b, _):
                _, use = misc.next(1 + K)
                act.wait_ge(misc_filled, use + 1)
                wait_from_one(act, bc_stored, b * 16)
                nc.scalar.copy(x_dbl[:], misc_ps[0:R + 2 * NS, :]).then_inc(misc_moved, 1)

            def ssm_exp(b, _):
                act.wait_ge(z_ready, (b + 1) * K)
                nc.scalar.activation(sp_e, sp_z[:], ACT.Abs).then_inc(sp_funcs, 1)
                act.wait_ge(sp_funcs, b * 2 + 1)
                nc.scalar.activation(sp_e, sp_e, ACT.Exp, scale=-1.0).then_inc(sp_funcs, 1)

            def ssm(b, g):
                c, n0 = g // (NS // GROUP), g % (NS // GROUP) * GROUP
                if n0 == 0:
                    act.wait_ge(z_steps, (b * K + c + 1) * ZS)
                if g == 0:
                    act.wait_ge(a_ready, 2)
                    act.wait_ge(dve_consts, 1)
                wait_from_one(act, scanned, b * GROUPS + max(g - 1, 0))
                for n in range(GROUP):
                    nc.scalar.activation(d_a[:, g % 2, n, 1:L], delta[:, c, 1:L], ACT.Exp,
                                         scale=a_col[:, c, n0 + n:n0 + n + 1]).then_inc(da_ready, 1)

            def ssm_out(b, _):
                wait_from_one(act, out_stored, b * 16)
                for j0 in range(0, J, 2):
                    move_turned(y_tok[:, j0:j0 + 2, :], lambda bank: bank[:].rearrange("p (j d) -> p j d", j=2))

            def gates_in(b, _):
                move_tiles(back_t, J)

            def gates(b, _):
                _, use = misc.next()
                act.wait_ge(misc_moved, use + 1)
                nc.scalar.activation(sc[:], sc[:], ACT.Exp).then_inc(gate_exp, 1)

            def places(b, _):
                wait_from_one(act, round_steps, b * RD)
                act.wait_ge(dve_consts, 4)
                move_turned(work[:, CAP:CAP + L], lambda bank: bank[0:E, :])

            def shared(b, m):
                half_tanh(SH_ROWS[m], 2 if m == 2 else 1)

            act.wait_ge(w_ssm_loaded, 16 * 5)
            nc.scalar.activation(a_col[:], a_col[:], ACT.Exp).then_inc(a_ready, 1)
            run(act, dict(attn_in=attn_in, attn_score=attn_score, route_gate=route_gate, ffn_in=ffn_in, ffn=ffn,
                          ffn_tail=ffn_tail, ssm_in=ssm_in, ssm_proj=ssm_proj, ssm_exp=ssm_exp, ssm=ssm,
                          ssm_out=ssm_out, gates_in=gates_in, gates=gates, places=places, shared=shared), [turn, misc, gu],
                [(misc, MISCS, ("ssm_proj", "gates"))])

            move_turned(ids_t, lambda bank: bank[:, 0:E])

            def move_rows(p, par):
                act.wait_ge(xg_turned, p + 1)
                nc.scalar.copy(xg_t[:, par, :, :], turn_ps[0][:, 0:K * P].rearrange("p (k t) -> p k t", k=K)
                               ).then_inc(xgt_ready, 1)

            def move_h1(p, par):
                act.wait_ge(h1_turned, p + 1)
                nc.scalar.copy(h1_t[:, par, :, :], turn_ps[1][0:FC, 0:2 * P].rearrange("p (c t) -> p c t", c=2)
                               ).then_inc(h1t_ready, 1)

            def pair(p, q, i):
                act.wait_ge(gu1_filled, p + 1)
                wait_from_one(act, h1_ready, p - 1)
                nc.scalar.activation(sig1[:, q % 2, :], gate_ps[q % 2][:, 0:F1], ACT.Tanh, scale=0.5
                                     ).then_inc(tanh1_ready, 1)
                if not isinstance(p, int) or p + 1 < PAIRS:
                    move_rows(p + 1, (q + 1) % 2)
                if not isinstance(p, int) or p >= 1:
                    move_h1(p - 1, (q - 1) % 2)

            move_rows(0, 0)
            run_pairs(act, pair)
            move_h1(PAIRS - 1, (PAIRS - 1) % 2)

        @block.vector
        def _(dve):
            turn, misc, gu, silu_ring = rings()
            tt, ts, stt = nc.vector.tensor_tensor, nc.vector.tensor_scalar, nc.vector.scalar_tensor_tensor
            reduce, recip = nc.vector.tensor_reduce, nc.vector.reciprocal

            def wide(ap, n):
                return ap.unsqueeze(2).broadcast_to([P, ap.shape[1], n])

            def norm(n, b, dst):
                s, w, mv = ln_steps[n], ln_w[n], ln_mv[n]
                for j in range(J):
                    nc.vector.bn_stats(ln_st[n][:, j, :], x_res[:, b * J + j, :]).then_inc(s, 1)
                wait_apart(dve, passed["dve"], (s, b * LN + J))
                for j in range(J):
                    nc.vector.bn_aggr(mv[:, j, :], ln_st[n][:, j, :]).then_inc(s, 1)
                dve.wait_ge(s, b * LN + 2 * J)
                ts(w[:, 0, :], mv[:, :, 1], EPS, None, ALU.add).then_inc(s, 1)
                dve.wait_ge(s, b * LN + 2 * J + 1)
                v, t, r = (w[:, row, :] for row in range(3))
                ts(t.bitcast(I32), v.bitcast(I32), 1, None, ALU.logical_shift_right).then_inc(s, 1)
                dve.wait_ge(s, b * LN + 2 * J + 2)
                ts(r.bitcast(I32), t.bitcast(I32), -1.0, float(HALF_EXPONENT), ALU.mult, ALU.add).then_inc(s, 1)
                for step in range(NEWTON):
                    dve.wait_ge(s, b * LN + 2 * J + 3 + 3 * step)
                    tt(t, r, r, ALU.mult).then_inc(s, 1)
                    dve.wait_ge(s, b * LN + 2 * J + 4 + 3 * step)
                    stt(out=t, in0=t, scalar=-0.5, in1=v, op0=ALU.mult, op1=ALU.mult).then_inc(s, 1)
                    dve.wait_ge(s, b * LN + 2 * J + 5 + 3 * step)
                    stt(out=r, in0=t, scalar=1.5, in1=r, op0=ALU.add, op1=ALU.mult).then_inc(s, 1)
                dve.wait_ge(s, b * LN + 2 * J + 3 + 3 * NEWTON)
                for j in range(J):
                    ts(dst[:, j, 0:D], x_res[:, b * J + j, :], mv[:, j, 0:1], r[:, j:j + 1],
                       ALU.subtract, ALU.mult).then_inc(s, 1)

            def attn_in(b, _):
                if isinstance(b, int):
                    for loaded in x_loaded:
                        dve.wait_ge(loaded, 16)
                    dve.wait_ge(w_attn_loaded, 16 * 5)
                    dve.wait_ge(pool_consts, 10)
                wait_from_one(dve, rows_sorted, b * 16 * J)
                norm(0, b, xn_f)

            def attn_qkv(b, _):
                for j in range(J):
                    _, use = misc.next()
                    dve.wait_ge(misc_filled, use + 1)
                    tt(qkv[:, j, :], misc_ps[:, 0:QKV], b_qkv[:], ALU.add).then_inc(misc_moved, 1)
                dve.wait_ge(misc_moved, use + 1)

            w4 = mix[:].rearrange("p j (h d) -> p j h d", h=H)
            score, best, diff, ex, den, rec, prob = (att_s[:, r, :] for r in range(7))

            def attn_score(b, _):
                q4 = qkv[:, :, 0:D].rearrange("p j (h d) -> p j h d", h=H)
                k4 = qkv[:, :, D:D + HD].unsqueeze(2).broadcast_to([P, J, H, HD])
                tt(w4, q4, k4, ALU.mult).then_inc(attn_steps, 1)
                dve.wait_ge(attn_steps, b * AT + 1)
                reduce(score, mix[:].rearrange("p j (h d) -> p (j h) d", h=H), AX, ALU.add).then_inc(attn_steps, 1)
                dve.wait_ge(attn_steps, b * AT + 2)
                reduce(best, score.unsqueeze(2), AX, ALU.max).then_inc(attn_steps, 1)
                dve.wait_ge(attn_steps, b * AT + 3)
                tt(diff, score, best, ALU.subtract).then_inc(attn_steps, 1)

            def attn_add(b, _):
                v4 = qkv[:, :, D + HD:QKV].unsqueeze(2).broadcast_to([P, J, H, HD])
                dve.wait_ge(attn_exp, b + 1)
                reduce(den, ex.unsqueeze(2), AX, ALU.add).then_inc(attn_steps, 1)
                dve.wait_ge(attn_steps, b * AT + 5)
                recip(rec, den).then_inc(attn_steps, 1)
                dve.wait_ge(attn_steps, b * AT + 6)
                tt(prob, ex, rec, ALU.mult).then_inc(attn_steps, 1)
                dve.wait_ge(attn_steps, b * AT + 7)
                tt(w4, v4, prob.rearrange("p (j h) -> p j h", j=J).unsqueeze(3).broadcast_to([P, J, H, HD]),
                   ALU.mult).then_inc(attn_steps, 1)
                dve.wait_ge(attn_steps, b * AT + 8)
                xb = x_res[:, bass.ds(b * J, J), :]
                tt(xb, xb, mix[:], ALU.add).then_inc(attn_steps, 1)
                wait_apart(dve, passed["dve"], (attn_steps, (b + 1) * AT))

            def route_gate(b, _):
                norm(1, b, xn_f)
                dve.wait_ge(ln_steps[1], (b + 1) * LN)
                s = route_steps
                for j in range(J):
                    for e in range(2):
                        nc.vector.tensor_tensor_reduce(out=(mix[:, j, :], front_t[:, j * D:(j + 1) * D])[e], in0=xn_f[:, j, :], in1=g0_row[:, e, :],
                                                       scale=1.0, scalar=0.0, op0=ALU.mult, op1=ALU.add,
                                                       accum_out=rt[:, 0, 2 * j + e:2 * j + e + 1]).then_inc(s, 1)
                dve.wait_ge(s, b * RT + 8)
                lg = rt[:, 0, :].rearrange("p (j e) -> p j e", e=2)
                best = rt[:, 1, 0:J]
                reduce(best, lg, AX, ALU.max).then_inc(s, 1)
                tt(rt[:, 6, 0:J], lg[:, :, 1], lg[:, :, 0], ALU.is_gt).then_inc(s, 1)
                dve.wait_ge(s, b * RT + 9)
                tt(rt[:, 2, :].rearrange("p (j e) -> p j e", e=2), lg, wide(best, 2), ALU.subtract).then_inc(s, 1)

            def route_slots(b, _):
                s = route_steps
                dve.wait_ge(route_exp, b + 1)
                ex = rt[:, 3, :].rearrange("p (j e) -> p j e", e=2)
                reduce(rt[:, 4, 0:J], ex, AX, ALU.add).then_inc(s, 1)
                reduce(rt[:, 4, J:2 * J], ex, AX, ALU.max).then_inc(s, 1)
                dve.wait_ge(s, b * RT + 13)
                recip(rt[:, 5, 0:J], rt[:, 4, 0:J]).then_inc(s, 1)
                dve.wait_ge(s, b * RT + 14)
                tt(rt[:, 5, J:2 * J], rt[:, 4, J:2 * J], rt[:, 5, 0:J], ALU.mult).then_inc(s, 1)
                _, use = misc.next()
                dve.wait_ge(misc_filled, use + 1)
                nc.vector.tensor_copy(rt[:, 7, :], misc_ps[:, 0:2 * J]).then_inc(misc_moved, 1)
                dve.wait_ge(misc_moved, use + 1)
                nc.vector.tensor_tensor_scan(rt[:, 8, 0:J], ones[:, 0:J], rt[:, 7, J:2 * J], 0.0,
                                             ALU.mult, ALU.add).then_inc(s, 1)
                tt(rt[:, 9, 0:J], rt[:, 7, 0:J], rt[:, 7, J:2 * J], ALU.subtract).then_inc(s, 1)
                tt(rt[:, 10, 0:J], rt[:, 6, 0:J], last_slot[:], ALU.mult).then_inc(s, 1)
                dve.wait_ge(s, b * RT + 18)
                tt(rt[:, 11, 0:J], rt[:, 9, 0:J], rt[:, 8, 0:J], ALU.add).then_inc(s, 1)
                dve.wait_ge(s, b * RT + 19)
                tt(rt[:, 12, 0:J], tok_local[:], rt[:, 11, 0:J], ALU.subtract).then_inc(s, 1)
                dve.wait_ge(s, b * RT + 20)
                wait_from_one(dve, yt_loaded, b * 16 * J)
                tt(slot_idx[:], rt[:, 12, 0:J], rt[:, 10, 0:J], ALU.add).then_inc(s, 1)
                ts(rt_ex[:], tile_thr[:], rt[0:1, 8, J - 1:J], None, ALU.is_le).then_inc(s, 1)

            def silu(rows, dst, uses):
                slot, use = gu.next(uses)
                _, n = silu_ring.next()
                dve.wait_ge(tanh_ready, n + 1)
                s = sig[0:rows, slot, :]
                stt(out=s, in0=s, scalar=1.0, in1=gate_ps[slot][0:rows, :], op0=ALU.add, op1=ALU.mult
                    ).then_inc(silu_steps, 1)
                dve.wait_ge(silu_steps, n + 1)
                w = 512 // uses
                for u in range(0, 512, w):
                    stt(out=dst[:, u:u + w], in0=s[:, u:u + w], scalar=0.5, in1=up_ps[slot][0:rows, u:u + w],
                        op0=ALU.mult, op1=ALU.mult).then_inc(gu_used, 1)

            def ffn(b, s):
                silu(P, h0[:, s % 2, :], 1)

            def ffn_out(b, _):
                dve.wait_ge(yt_loaded, (b + 1) * 16 * J)
                for j in range(J):
                    xt = x_res[:, b * J + j, :]
                    stt(out=xt, in0=mix[:, j, :], scalar=rt[:, 5, J + j:J + j + 1], in1=xt,
                        op0=ALU.mult, op1=ALU.add).then_inc(x_after_ffn, 1)
                wait_apart(dve, passed["dve"], (x_after_ffn, (b + 1) * J))

            def ssm_in(b, _):
                wait_apart(dve, passed["dve"], (table_stored, b * 16))
                norm(2, b, xf)

            def ssm_proj(b, _):
                misc.next()
                for c in range(K):
                    _, use = misc.next()
                    dve.wait_ge(misc_filled, use + 1)
                    ts(sp_z[:, c, :], misc_ps[:], bdt_col[:, c:c + 1], None, ALU.add).then_inc(misc_moved, 1)
                dve.wait_ge(misc_moved, use + 1)
                dve.sem_inc(z_ready, K)

            def ssm_delta(b, c):
                s, done = z_steps, (b * K + c) * ZS
                e, d = sp_e[:, c, :], delta[:, c, :]
                dve.wait_ge(sp_funcs, b * 2 + 2)
                ts(d, e, LOG1P[-1], None, ALU.mult).then_inc(s, 1)
                for k in range(len(LOG1P) - 2, -1, -1):
                    dve.wait_ge(s, done + len(LOG1P) - 1 - k)
                    stt(out=d, in0=d, scalar=LOG1P[k], in1=e, op0=ALU.add, op1=ALU.mult).then_inc(s, 1)
                dve.wait_ge(s, done + len(LOG1P))
                stt(out=d, in0=sp_z[:, c, :], scalar=0.0, in1=d, op0=ALU.max, op1=ALU.add).then_inc(s, 1)

            def ssm(b, g):
                c, quarter = g // (NS // GROUP), g % (NS // GROUP)
                flat = "p n l -> p (n l)"
                buf = hs[:, g % 2, :, :]
                dve.wait_ge(da_ready, b * GROUPS * GROUP + GROUP * g + GROUP)
                dve.wait_ge(dbu_ready, b * GROUPS + g + 1)
                nc.vector.tensor_tensor_scan(buf.rearrange(flat), d_a[:, g % 2, :, :].rearrange(flat),
                                             buf.rearrange(flat), 0.0, ALU.mult, ALU.add).then_inc(scanned, 1)
                n0 = NS + quarter * GROUP
                dve.wait_ge(scanned, b * GROUPS + g + 1)
                tt(buf, buf, bc[:, n0:n0 + GROUP, :], ALU.mult).then_inc(hc_ready, 1)
                dve.wait_ge(hc_ready, b * GROUPS + g + 1)
                if quarter == 0:
                    tt(y_fm[:, c, :], hs[:, g % 2, 0, :], hs[:, g % 2, 1, :], ALU.add).then_inc(group_summed, 1)
                else:
                    tt(y_half[:], hs[:, g % 2, 0, :], hs[:, g % 2, 1, :], ALU.add).then_inc(sum_steps, 1)
                    dve.wait_ge(sum_steps, b * (GROUPS - K) + g - c)
                    dve.wait_ge(group_summed, b * GROUPS + g)
                    tt(y_fm[:, c, :], y_fm[:, c, :], y_half[:], ALU.add).then_inc(group_summed, 1)

            def ssm_out(b, _):
                _, use = turn.next(2)
                dve.wait_ge(turn_moved, use + 2)
                dve.wait_ge(skip_steps, (b + 1) * 2)
                xb = x_res[:, bass.ds(b * J, J), :]
                tt(xb, xb, y_tok, ALU.add).then_inc(x_after_ssm, 1)
                wait_apart(dve, passed["dve"], (x_after_ssm, b + 1))

            def gates_in(b, _):
                norm(3, b, xf)

            def gates(b, _):
                _, use = misc.next()
                s = gate_steps
                dve.wait_ge(misc_filled, use + 1)
                lg = misc_ps[:, 0:J * E].rearrange("p (j e) -> p j e", j=J)
                reduce(sc_s[:, 0, :], lg, AX, ALU.max).then_inc(s, 1)
                dve.wait_ge(s, b * GT + 1)
                tt(sc[:], lg, wide(sc_s[:, 0, :], E), ALU.subtract).then_inc(misc_moved, 1)
                dve.wait_ge(gate_exp, b + 1)
                reduce(sc_s[:, 1, :], sc[:], AX, ALU.add).then_inc(s, 1)
                dve.wait_ge(s, b * GT + 2)
                recip(sc_s[:, 2, :], sc_s[:, 1, :]).then_inc(s, 1)
                dve.wait_ge(s, b * GT + 3)
                wait_from_one(dve, scores_copied, b)
                tt(sc66[:, :, 0:E], sc[:], wide(sc_s[:, 2, :], E), ALU.mult).then_inc(s, 1)
                wait_apart(dve, passed["dve"], (s, (b + 1) * GT))

            def places(b, _):
                s = top_steps
                dve.wait_ge(dve_consts, 4)
                for j in range(J):
                    nc.vector.max(top[:, j, :], sc66[:, j, :]).then_inc(s, 1)
                dve.wait_ge(s, b * TOP + J)
                nc.vector.memset(top[:, :, TOPK:TOPK + 1], -1.0).then_inc(s, 1)
                nc.vector.memset(top[:, :, TOPK + 1:TOPK + 2], -2.0).then_inc(s, 1)
                wait_apart(dve, passed["dve"], (s, b * TOP + J + 2))
                for j in range(J):
                    nc.vector.match_replace(out=marked[:, j, :], in_to_replace=top[:, j, :], in_values=sc66[:, j, :],
                                            imm_value=-3.0).then_inc(s, 1)
                dve.wait_ge(s, b * TOP + 2 * J + 2)
                stt(out=marked[:, :, 0:E], in0=marked[:, :, 0:E], scalar=-3.0,
                    in1=wide(tok_value[:, bass.ds(b * J, J)], E), op0=ALU.is_equal, op1=ALU.mult).then_inc(s, 1)

            def rounds(b, first, last):
                s = round_steps
                for r in range(first, last):
                    nc.vector.max(keep[:, 8 * r:8 * r + 8], work[:]).then_inc(s, 1)
                    wait_apart(dve, passed["dve"], (s, b * RD + 2 * r + 1))
                    nc.vector.match_replace(out=work[:], in_to_replace=keep[:, 8 * r:8 * r + 8], in_values=work[:],
                                            imm_value=0.0).then_inc(s, 1)
                    wait_apart(dve, passed["dve"], (s, b * RD + 2 * r + 2))
                if last == ROUNDS:
                    nc.vector.tensor_copy(work[:, 0:CAP], keep[:]).then_inc(s, 1)
                    dve.wait_ge(s, (b + 1) * RD)

            def shared(b, m):
                silu(SH_ROWS[m], hsh_t[0:SH_ROWS[m], m, :], 2 if m == 2 else 1)
                if m == 0:
                    wait_apart(dve, passed["dve"], (turn_moved, turn.so_far()))
                rounds(b, m * ROUNDS // 3, (m + 1) * ROUNDS // 3)

            def shared_out(b, _):
                for j0 in range(0, J, 2):
                    _, use = misc.next()
                    dve.wait_ge(misc_filled, use + 1)
                    tt(o_sb[:, j0:j0 + 2, :], x_res[:, bass.ds(b * J + j0, 2), :],
                       misc_ps[:].rearrange("p (j d) -> p j d", j=2), ALU.add).then_inc(misc_moved, 1)

            nc.vector.memset(d_a[:], 0.0).then_inc(dve_consts, 1)
            nc.vector.memset(work[:], 0.0).then_inc(dve_consts, 1)
            nc.vector.memset(sc66[:, :, E:E + 1], -1.0).then_inc(dve_consts, 1)
            nc.vector.memset(sc66[:, :, E + 1:E + 2], -2.0).then_inc(dve_consts, 1)
            dve.wait_ge(a_ready, 1)
            ts(a_col[:], a_col[:], -1.0, None, ALU.mult).then_inc(a_ready, 1)
            run(dve, dict(attn_in=attn_in, attn_qkv=attn_qkv, attn_score=attn_score, attn_add=attn_add,
                          route_gate=route_gate, route_slots=route_slots, ffn=ffn, ffn_out=ffn_out,
                          ssm_in=ssm_in, ssm_proj=ssm_proj, ssm_delta=ssm_delta, ssm=ssm, ssm_out=ssm_out,
                          gates_in=gates_in, gates=gates, places=places, shared=shared, shared_out=shared_out),
                [turn, misc, gu, silu_ring], [(turn, TURNS, ("ssm_out",))])

            stt(out=ids_z[:], in0=keep[:], scalar=0.0, in1=place_no[:], op0=ALU.is_equal, op1=ALU.mult
                ).then_inc(ids_steps, 1)
            dve.wait_ge(ids_steps, 1)
            for half in range(2):
                stt(out=ids[:, half, :], in0=ids_z[:], scalar=float(N), in1=keep[:], op0=ALU.add, op1=ALU.subtract
                    ).then_inc(ids_steps, 1)
            turn.next()
            dve.wait_ge(turn_moved, turn.so_far())
            by_pair = ids_t.rearrange("p (n e) -> p n e", e=2)
            for e in range(2):
                rows = slice(e * CAP, (e + 1) * CAP)
                nc.vector.tensor_copy(idx_get[rows, :], by_pair[rows, :, e]).then_inc(ids_steps, 1)
            nc.vector.tensor_copy(idx_add[:], ids_t[0:CAP, :]).then_inc(ids_steps, 1)

            def weigh(p, slot):
                par = slot % 2
                dve.wait_ge(down1_filled, p + 1)
                for added in rows_added:
                    wait_from_one(dve, added, 16 * (p - 1))
                for e in range(2):
                    rows = slice(e * CAP, (e + 1) * CAP)
                    col = D + e + 2 * p
                    ts(yo[rows, par, :], y_ps[par][rows, 0:D], xg[slot][rows, bass.ds(col, 1)], None,
                       ALU.mult).then_inc(yo_halves, 1)

            def pair(p, q, i):
                par = q % 2
                s = sig1[:, par, :]
                dve.wait_ge(tanh1_ready, p + 1)
                stt(out=s, in0=s, scalar=1.0, in1=gate_ps[par][:, 0:F1], op0=ALU.add, op1=ALU.mult
                    ).then_inc(silu1_steps, 1)
                dve.wait_ge(silu1_steps, p + 1)
                stt(out=h1[:, par, :], in0=s, scalar=0.5, in1=gate_ps[par][:, F1:FSH], op0=ALU.mult, op1=ALU.mult
                    ).then_inc(h1_ready, 1)
                if not isinstance(p, int) or p >= 2:
                    weigh(p - 2, (q - 2) % ROW_RING)

            run_pairs(dve, pair)
            weigh(PAIRS - 2, (PAIRS - 2) % ROW_RING)
            weigh(PAIRS - 1, (PAIRS - 1) % ROW_RING)


def kernel(**inputs):
    import numpy as np
    import concourse.bacc as bacc
    from concourse.bass_utils import run_bass_kernel_spmd

    def arr(name, *axes):
        a = np.asarray(inputs[name])
        return np.ascontiguousarray(a.transpose(axes) if axes else a)

    arrays = {
        "x": arr("L0_attn_x").reshape(N, D),
        "wq_t": arr("L0_attn_Wq", 1, 0), "bq": arr("L0_attn_bq"),
        "wkv_t": arr("L0_attn_Wkv", 1, 0), "bkv": arr("L0_attn_bkv"),
        "gate0": arr("L0_ffn_gate_w"),
        "wg0_t": arr("L0_ffn_w_gate", 0, 2, 1), "wu0_t": arr("L0_ffn_w_up", 0, 2, 1),
        "wd0_t": arr("L0_ffn_w_down", 0, 2, 1),
        "wx_t": arr("L1_attn_W_xproj", 1, 0), "wdt_t": arr("L1_attn_W_dt", 1, 0),
        "b_dt": np.ascontiguousarray(arr("L1_attn_b_dt").reshape(K, P).T), "a_log": arr("L1_attn_A_log"), "d_par": arr("L1_attn_D_param"),
        "gate1_t": arr("L1_ffn_gate_w", 1, 0),
        "wg1": arr("L1_ffn_w_gate"), "wu1": arr("L1_ffn_w_up"), "wd1": arr("L1_ffn_w_down"),
        "shg_t": arr("L1_ffn_sh_gate", 1, 0), "shu_t": arr("L1_ffn_sh_up", 1, 0),
        "shd_t": arr("L1_ffn_sh_down", 1, 0),
    }
    nc = bacc.Bacc("TRN2", target_bir_lowering=False, num_devices=1)
    args = [nc.dram_tensor(f"in_{n}", a.shape, mybir.dt.from_np(a.dtype), kind="ExternalInput").ap()
            for n, a in arrays.items()]
    args.append(nc.dram_tensor("out_rows", (ROWS, D), F32, kind="ExternalOutput").ap())
    build(nc, *args)
    r = run_bass_kernel_spmd(nc, [{f"in_{n}": a for n, a in arrays.items()}], core_ids=[0])
    return r.results[0]["out_rows"][0:N].reshape(B, L, D)
```

```python
from contextlib import ExitStack

import concourse.bass as bass
from concourse import mybir

F32 = mybir.dt.float32
U32 = mybir.dt.uint32
I32 = mybir.dt.int32
ALU = mybir.AluOpType
ACT = mybir.ActivationFunctionType
AX = mybir.AxisListType.X

P = 128
B, L, D = 4, 512, 256
N = B * L
J = L // P
K = D // P
H, HD = 16, 16
QKV = D + 2 * HD
FF = 1024
HALF = FF // 512
S0 = J + 1
SLOTS = S0 * P
STEPS = S0 * HALF
NS = 8
R = D // 8
GROUP = 2
GROUPS = K * NS // GROUP
C_ON_VECTOR = (B - 2, B - 1)
E, CAP, TOPK, F1 = 64, 64, 6, 176
FC = F1 // 2
PAIRS = E // 2
RING = 8
RING_IN_BIG = 5
ROW_RING = 8
FSH = 2 * F1
SH_ROWS = [128, 128, FSH - 256]
XW = D + E
ROWS = N + CAP
EPS = 1e-5
HALF_EXPONENT = 0x5F3759DF
NEWTON = 3
LN = 3 * J + 3 + 3 * NEWTON
AT_DIFF, AT = J + 4, J + 9
RT_SEL, RT_DIFF, RT = 10, 11, 22
LOG1P = [0.999999995, -0.49999904, 0.33330004, -0.249545589, 0.196781173, -0.153118631, 0.106142647,
         -0.0570642008, 0.019907161, -0.00325637848]
ZS = len(LOG1P) + 1
GT = 4
TOP = 2 * J + 3
ROUNDS = CAP // 8
RD = 2 * ROUNDS + 1


class Ring:

    def __init__(self, slots):
        self.slots, self.k, self.wide = slots, 0, False

    def next(self, uses=1):
        k = self.k
        self.free_at = k - (0 if self.wide else 1)
        self.wide = uses > 1
        self.k += uses
        return k % self.slots, k

    def so_far(self):
        return self.k


def wait_from_one(eng, sem, count):
    if not isinstance(count, int) or count > 0:
        eng.wait_ge(sem, count)


def wait_apart(eng, passed, *waits):
    for sem, value in waits:
        wait_from_one(eng, sem, value)
    if any(not isinstance(v, int) for _, v in waits):
        eng.sem_inc(passed, 1)


def build(nc, x, wq_t, bq, wkv_t, bkv, gate0, wg0_t, wu0_t, wd0_t, wx_t, wdt_t, b_dt, a_log, d_par,
          gate1_t, wg1, wu1, wd1, shg_t, shu_t, shd_t, out):
    with ExitStack() as ctx:
        def sb(name, shape, dt=F32):
            return ctx.enter_context(nc.sbuf_tensor(name, shape, dt))

        def ps(name):
            return ctx.enter_context(nc.psum_tensor(name, [P, 512], F32))

        def sem(name):
            return ctx.enter_context(nc.semaphore(name))

        x_res = sb("x_res", [P, B * J, D])
        ident = sb("ident", [P, P])
        before_me = sb("before_me", [P, P])
        ones = sb("ones", [P, P])
        tok_local = sb("tok_local", [P, J])
        last_slot = sb("last_slot", [P, J])
        tok_value = sb("tok_value", [P, B * J])
        tile_thr = sb("tile_thr", [1, S0])
        place_no = sb("place_no", [CAP, CAP])

        w_qkv = sb("w_qkv", [P, K, QKV])
        b_qkv = sb("b_qkv", [P, QKV])
        g0_row = sb("g0_row", [P, 2, D])
        big = sb("big", [P, 2 * K * 2 * FF + 2 * 8 * D])
        gu0 = big[:, 0:2 * K * 2 * FF].rearrange("p (e k g f) -> p e k g f", e=2, k=K, g=2)
        dn0 = big[:, 2 * K * 2 * FF:].rearrange("p (e c d) -> p e c d", e=2, c=8)
        front_sizes = dict(xn_f=J * D, front_t=K * S0 * P, xn_t=K * J * P, act_buf=4 * 512, mix=J * D, xs=S0 * D)
        front_area = sb("front_area", [P, sum(front_sizes.values())])
        in_front, start = {}, 0
        for name, size in front_sizes.items():
            in_front[name] = front_area[:, start:start + size]
            start += size
        pair_size = 4 * FSH + 4 * D
        gu1, dn1 = [], []
        for q in range(RING):
            area, n = (big, q) if q < RING_IN_BIG else (front_area, q - RING_IN_BIG)
            at_gu, at_dn = n * pair_size, n * pair_size + 4 * FSH
            gu1.append(area[:, at_gu:at_dn].rearrange("p (a f) -> p a f", a=4))
            dn1.append(area[0:FC, at_dn:at_dn + 4 * D].rearrange("p (a d) -> p a d", a=4))
        w_x = sb("w_x", [P, K, R + 2 * NS])
        w_dt = sb("w_dt", [R, D])
        bdt_col = sb("bdt_col", [P, K])
        a_col = sb("a_col", [P, K, NS])
        d_row = sb("d_row", [P, D])
        w_g1 = sb("w_g1", [P, K, E])
        w_sh = sb("w_sh", [P, K, 2, FSH])
        w_shd = sb("w_shd", [P, 3, D])

        ln_st = [sb(f"ln_st{i}", [P, J, 6]) for i in range(4)]
        ln_mv = [sb(f"ln_mv{i}", [P, J, 2]) for i in range(4)]
        ln_w = [sb(f"ln_w{i}", [P, 3, J]) for i in range(4)]

        xn_f = in_front["xn_f"].rearrange("p (j d) -> p j d", j=J)
        front_t = in_front["front_t"]
        xn_t = in_front["xn_t"]
        xn_attn_t = xn_t.rearrange("p (k j t) -> p k j t", k=K, j=J)
        xs_t = front_t.rearrange("p (k j t) -> p k j t", k=K, j=S0)
        act_buf = in_front["act_buf"]
        h0 = act_buf[:, 0:1024].rearrange("p (s f) -> p s f", s=2)
        h0_t = act_buf[:, 1024:2048].rearrange("p (s f) -> p s f", s=2)
        kv = sb("kv", [P, J, 2 * HD])
        att_s = sb("att_s", [P, 7, J * H])
        mix = in_front["mix"].rearrange("p (j d) -> p j d", j=J)
        rt = sb("rt", [P, 13, 2 * J])
        rt_ex = sb("rt_ex", [1, S0], I32)
        slot_new = sb("slot_new", [P, J], U32)
        slot_idx = sb("slot_idx", [P, J], U32)
        slot_w = sb("slot_w", [P, J])
        xs = in_front["xs"].rearrange("p (s d) -> p s d", s=S0)
        sig = sb("sig", [P, 2, 512])

        xf = sb("xf", [P, J, XW])
        back_t = sb("back_t", [P, K, J, P])
        y_fm = back_t[:].rearrange("p k j t -> p k (j t)")
        x_dbl = sb("x_dbl", [R + 2 * NS, L])
        bc = sb("bc", [P, 2 * NS, L])
        sp_z = sb("sp_z", [P, K, L])
        hsh_t = sb("hsh_t", [P, 3, L])
        sp_e = hsh_t[:, 0:K, :]
        io_buf = sb("io_buf", [P, J * D])
        y_tok = io_buf[:].rearrange("p (j d) -> p j d", j=J)
        o_sb = y_tok
        q_buf = y_tok
        delta = sb("delta", [P, K, L])
        d_a = sb("d_a", [P, 2, GROUP, L])
        hs = sb("hs", [P, 2, GROUP, L])
        y_half = sb("y_half", [P, L])
        sc = sb("sc", [P, J, E])
        sc66 = sb("sc66", [P, J, E + 2])
        sc_s = sb("sc_s", [P, 3, J])
        top = sb("top", [P, J, 8])
        marked = sb("marked", [P, J, E + 2])
        work = sb("work", [CAP, CAP + L])
        keep = sb("keep", [CAP, CAP])

        ids = sb("ids", [CAP, 2, CAP])
        ids_z = sb("ids_z", [CAP, CAP])
        idx_get = sb("idx_get", [P, PAIRS], U32)
        idx_add = sb("idx_add", [CAP, E], U32)
        area = bc[:].rearrange("p n l -> p (n l)")
        at = [0]

        def carve(n):
            at[0] += n
            return area[:, at[0] - n:at[0]]

        ids_t = carve(E)
        xg = [carve(XW) for _ in range(ROW_RING)]
        xg_t = carve(2 * K * P).rearrange("p (s k t) -> p s k t", s=2, k=K)
        sig1 = carve(2 * F1).rearrange("p (s f) -> p s f", s=2)
        h1 = carve(2 * F1).rearrange("p (s f) -> p s f", s=2)
        h1_t = carve(4 * P)[0:FC, :].rearrange("p (s c t) -> p s c t", s=2, c=2)
        yo = carve(2 * D).rearrange("p (s d) -> p s d", s=2)
        clear = carve(XW)

        gate_ps = [ps("gate_ps0"), ps("gate_ps1")]
        up_ps = [ps("up_ps0"), ps("up_ps1")]
        turn_ps = [ps("turn_ps0"), ps("turn_ps1")]
        down_ps = ps("down_ps")
        misc_ps = ps("misc_ps")

        y_ps = [down_ps, misc_ps]

        sorted_dram = nc.dram_tensor("sorted_dram", (SLOTS, D), F32).ap()
        ysorted_dram = nc.dram_tensor("ysorted_dram", (SLOTS, D), F32).ap()
        bc_dram = nc.dram_tensor("bc_dram", (2 * NS, L), F32).ap()
        table = nc.dram_tensor("table", (ROWS, XW), F32).ap()
        odd_out = nc.dram_tensor("odd_out", (ROWS, D), F32).ap()

        x_loaded = [sem(f"x_loaded{b}") for b in range(B)]
        w_attn_loaded = sem("w_attn_loaded")
        w_ffn_loaded = sem("w_ffn_loaded")
        w_ssm_loaded = sem("w_ssm_loaded")
        w_tail_loaded = sem("w_tail_loaded")
        pool_consts = sem("pool_consts")
        dve_consts = sem("dve_consts")
        a_ready = sem("a_ready")
        scratch_clear = sem("scratch_clear")
        turn_filled = sem("turn_filled")
        turn_moved = sem("turn_moved")
        misc_filled = sem("misc_filled")
        misc_moved = sem("misc_moved")
        gu_filled = sem("gu_filled")
        gu_used = sem("gu_used")
        down_filled = sem("down_filled")
        down_moved = sem("down_moved")
        tanh_ready = sem("tanh_ready")
        silu_steps = sem("silu_steps")
        ln_steps = [sem(f"ln_steps{i}") for i in range(4)]
        attn_steps = sem("attn_steps")
        attn_exp = sem("attn_exp")
        route_steps = sem("route_steps")
        route_exp = sem("route_exp")
        rows_sorted = sem("rows_sorted")
        slot_kept = sem("slot_kept")
        sorted_loaded = sem("sorted_loaded")
        ys_stored = sem("ys_stored")
        yt_loaded = sem("yt_loaded")
        x_after_ffn = sem("x_after_ffn")
        bc_stored = sem("bc_stored")
        bc_loaded = sem("bc_loaded")
        z_ready = sem("z_ready")
        z_steps = sem("z_steps")
        sp_funcs = sem("sp_funcs")
        du_ready = sem("du_ready")
        skip_steps = sem("skip_steps")
        da_ready = sem("da_ready")
        dbu_ready = sem("dbu_ready")
        scanned = sem("scanned")
        hc_ready = sem("hc_ready")
        sum_steps = sem("sum_steps")
        group_summed = sem("group_summed")
        x_after_ssm = sem("x_after_ssm")
        gate_steps = sem("gate_steps")
        gate_exp = sem("gate_exp")
        scores_copied = sem("scores_copied")
        top_steps = sem("top_steps")
        round_steps = sem("round_steps")
        table_stored = sem("table_stored")
        out_stored = sem("out_stored")
        ids_steps = sem("ids_steps")
        pair_loaded = [sem(f"pair_loaded{i}") for i in range(RING)]
        xg_loaded = [sem(f"xg_loaded{i}") for i in range(ROW_RING)]
        xg_turned = sem("xg_turned")
        xgt_ready = sem("xgt_ready")
        gu1_filled = sem("gu1_filled")
        tanh1_ready = sem("tanh1_ready")
        silu1_steps = sem("silu1_steps")
        h1_ready = sem("h1_ready")
        h1_turned = sem("h1_turned")
        h1t_ready = sem("h1t_ready")
        down1_filled = sem("down1_filled")
        yo_halves = sem("yo_halves")
        rows_added = [sem("even_rows_added"), sem("odd_rows_added")]
        sums_added = sem("sums_added")

        passed = {e: sem(f"passed_{e}") for e in ("sp", "pool", "pe", "dve")}

        order = [("F", "ffn_in"), ("B", "ssm_in"), ("R", "rounds", 0), ("A", "attn_in"), ("B", "ssm_proj"),
                 ("B", "ssm_exp"), ("F", "ffn", 0), ("A", "attn_turn"), ("L", "weights_ahead"),
                 ("B", "ssm_delta", 0), ("F", "ffn", 1),
                 ("B", "ssm", 0), ("A", "attn_qkv"),
                 ("F", "ffn", 2), ("B", "ssm", 1), ("B", "ssm_delta", 1), ("F", "ffn", 3), ("B", "ssm", 2),
                 ("A", "attn_score"), ("F", "ffn", 4), ("B", "ssm", 3), ("A", "attn_add"),
                 ("F", "ffn", 5), ("B", "ssm", 4), ("A", "route_gate"), ("F", "ffn", 6), ("B", "ssm", 5),
                 ("F", "ffn", 7), ("A", "route_slots"), ("B", "ssm", 6),
                 ("F", "ffn", 8), ("B", "ssm", 7), ("F", "ffn", 9),
                 ("B", "ssm_skip"), ("R", "rounds", 1), ("B", "ssm_out"), ("F", "ffn_tail"), ("B", "gates_in"),
                 ("R", "rounds", 2), ("B", "gates"), ("B", "places"), ("B", "shared", 0), ("L", "rounds", 0),
                 ("F", "ffn_out"), ("A", "ffn_load"), ("B", "shared", 1), ("L", "rounds", 1), ("L", "rounds", 2),
                 ("L", "tables"), ("B", "shared", 2), ("N", "ssm_norm"), ("B", "shared_out")]
        order = [(*stage, 0)[0:3] for stage in order]
        AHEAD = {"A": 2, "F": 1, "B": 0, "R": -1, "L": 0, "N": 1}
        TURNS = dict(attn_turn=2, ffn_in=3, ffn=1, ffn_tail=1, ssm_in=2, ssm_out=2, gates_in=2, places=1,
                     tables=1)
        MISCS = dict(attn_qkv=J, route_slots=1, ssm_proj=1 + K, gates=1, shared_out=2)

        def in_stage(uses, name, s):
            return 0 if name == "ffn" and s == 0 else uses.get(name, 0)

        def rings():
            return Ring(2), Ring(1), Ring(2), Ring(1)

        def run(eng, stages, skips=()):
            def turn_of(batch, sides):
                for side, name, s in order:
                    if side not in sides:
                        continue
                    for ring, uses, mine in skips:
                        if name not in mine and in_stage(uses, name, s):
                            ring.next(uses[name])
                    if name in stages:
                        stages[name](batch + AHEAD[side], s)

            batches = {"A": range(B), "F": range(B), "B": range(B), "R": range(B - 1), "L": [B - 1],
                       "N": range(B)}
            for turn_no in range(-2, B):
                turn_of(turn_no, [side for side in AHEAD if turn_no + AHEAD[side] in batches[side]])

        def run_pairs(eng, part):
            last = PAIRS // ROW_RING - 1
            for q in range(ROW_RING):
                part(q, q, 0)
            with eng.Fori(1, last) as i:
                for q in range(ROW_RING):
                    part(i * ROW_RING + q, q, i)
            for q in range(ROW_RING):
                part(ROW_RING * last + q, q, last)

        block = ctx.enter_context(nc.Block())

        @block.sync
        def _(sp):
            _, misc, _, _ = rings()

            def row(v, n):
                return v.rearrange("(o n) -> o n", o=1).broadcast_to([P, n])

            xv = x.rearrange("(t p) d -> p t d", p=P)
            sp.dma_start(x_res[:, 0:J, :], xv[:, 0:J, :]).then_inc(x_loaded[0], 16)
            sp.dma_start(w_qkv[:, :, 0:D], wq_t.rearrange("(k p) n -> p k n", p=P)).then_inc(w_attn_loaded, 16)
            sp.dma_start(w_qkv[:, :, D:QKV], wkv_t.rearrange("(k p) n -> p k n", p=P)).then_inc(w_attn_loaded, 16)
            sp.dma_start(b_qkv[:, 0:D], row(bq, D)).then_inc(w_attn_loaded, 16)
            sp.dma_start(b_qkv[:, D:QKV], row(bkv, 2 * HD)).then_inc(w_attn_loaded, 16)
            sp.dma_start(g0_row[:].rearrange("p e d -> p (e d)"),
                         row(gate0.rearrange("e d -> (e d)"), 2 * D)).then_inc(w_attn_loaded, 16)
            for e in range(2):
                for g, w in ((0, wg0_t), (1, wu0_t)):
                    sp.dma_start(gu0[:, e, :, g, :], w[e].rearrange("(k p) f -> p k f", p=P)
                                 ).then_inc(w_ffn_loaded, 16)
                sp.dma_start(dn0[:, e, :, :], wd0_t[e].rearrange("(c p) d -> p c d", p=P)).then_inc(w_ffn_loaded, 16)
            for b in range(1, B):
                sp.dma_start(x_res[:, b * J:(b + 1) * J, :], xv[:, b * J:(b + 1) * J, :]).then_inc(x_loaded[b], 16)
            sp.dma_start(a_col[:], a_log.rearrange("(k p) n -> p k n", p=P)).then_inc(w_ssm_loaded, 16)
            sp.dma_start(w_x[:], wx_t.rearrange("(k p) n -> p k n", p=P)).then_inc(w_ssm_loaded, 16)
            sp.dma_start(w_dt[:], wdt_t).then_inc(w_ssm_loaded, 16)
            sp.dma_start(bdt_col[:], b_dt).then_inc(w_ssm_loaded, 16)
            sp.dma_start(d_row[:], row(d_par, D)).then_inc(w_ssm_loaded, 16)
            sp.dma_start(w_g1[:], gate1_t.rearrange("(k p) n -> p k n", p=P)).then_inc(w_tail_loaded, 16)
            for g, w in ((0, shg_t), (1, shu_t)):
                sp.dma_start(w_sh[:, :, g, :], w.rearrange("(k p) f -> p k f", p=P)).then_inc(w_tail_loaded, 16)
            sp.dma_start(w_shd[:, 0:2, :], shd_t[0:256, :].rearrange("(c p) d -> p c d", p=P)).then_inc(w_tail_loaded, 16)
            sp.dma_start(w_shd[0:SH_ROWS[2], 2, :], shd_t[256:FSH, :]).then_inc(w_tail_loaded, 16)

            def ffn_load(b, _):
                wait_apart(sp, passed["sp"], (rows_sorted, (b + 1) * 16 * J))
                wait_apart(sp, passed["sp"], (x_after_ffn, b * J))
                sp.dma_start(xs, sorted_dram.rearrange("(s p) d -> p s d", p=P)).then_inc(sorted_loaded, 16)

            def ffn_out(b, _):
                wait_apart(sp, passed["sp"], (down_moved, (b + 1) * S0))
                wait_apart(sp, passed["sp"], (yt_loaded, b * 16 * J))
                sp.dma_start(ysorted_dram.rearrange("(s p) d -> p s d", p=P), xs).then_inc(ys_stored, 16)

            def ssm_proj(b, _):
                _, use = misc.next(1 + K)
                wait_apart(sp, passed["sp"], (misc_moved, use + 1))
                sp.dma_start(bc_dram, x_dbl[R:R + 2 * NS, :]).then_inc(bc_stored, 16)
                wait_apart(sp, passed["sp"], (bc_stored, (b + 1) * 16))
                wait_apart(sp, passed["sp"], (hc_ready, b * GROUPS))
                sp.dma_start(bc[:].rearrange("p n l -> p (n l)"),
                             bc_dram.rearrange("(o n) l -> o (n l)", o=1).broadcast_to([P, 2 * NS * L])
                             ).then_inc(bc_loaded, 16)

            def places(b, _):
                wait_apart(sp, passed["sp"], (scores_copied, b + 1))
                sp.dma_start(table[0:N, :].rearrange("(b j p) d -> p b j d", b=B, p=P)[:, b, :, :],
                             xf[:]).then_inc(table_stored, 16)

            def shared_out(b, _):
                _, use = misc.next(2)
                wait_apart(sp, passed["sp"], (misc_moved, use + 2))
                sp.dma_start(out[0:N, :].rearrange("(b j p) d -> p b j d", b=B, p=P)[:, b, :, :],
                             o_sb).then_inc(out_stored, 16)

            def weights(p, q, i):
                if isinstance(p, int) and p < RING_IN_BIG:
                    sp.wait_ge(down_filled, B * S0)
                elif isinstance(p, int) and p < RING:
                    sp.wait_ge(x_after_ffn, B * J)
                else:
                    wait_apart(sp, passed["sp"], (down1_filled, p - RING + 1))
                for g, w in ((0, wg1), (1, wu1)):
                    sp.dma_start(gu1[q % RING][:, :, g * F1:(g + 1) * F1],
                                 w.rearrange("(n e) (k p) f -> p n (e k) f", e=2, p=P)[:, p, :, :]
                                 ).then_inc(pair_loaded[q % RING], 16)
                sp.dma_start(dn1[q % RING], wd1.rearrange("(n e) (c p) d -> p n (e c) d", e=2, p=FC)[:, p, :, :]
                             ).then_inc(pair_loaded[q % RING], 16)

            def weights_ahead(b, _):
                for q in range(RING):
                    weights(q, q, 0)

            sp.wait_ge(scratch_clear, 64)
            run(sp, dict(ffn_load=ffn_load, ffn_out=ffn_out, ssm_proj=ssm_proj, places=places, shared_out=shared_out,
                         weights_ahead=weights_ahead),
                [(misc, MISCS, ("ssm_proj", "shared_out"))])

            with sp.Fori(1, PAIRS // RING) as i:
                for q in range(RING):
                    weights(i * RING + q, q, i)
            sp.wait_ge(out_stored, 16 * B)
            for added in rows_added:
                sp.wait_ge(added, 16 * PAIRS)
            sp.wait_ge(sums_added, 16)

        @block.gpsimd
        def _(pool):
            tt = nc.gpsimd.tensor_tensor

            nc.gpsimd.memset(clear, 0.0).then_inc(pool_consts, 1)
            nc.gpsimd.memset(ones[:], 1.0).then_inc(pool_consts, 1)
            nc.gpsimd.memset(ident[:], 0.0).then_inc(pool_consts, 1)
            pool.wait_ge(pool_consts, 3)
            nc.gpsimd.affine_select(out=ident[:], in_=ident[:], compare_op=ALU.not_equal, fill=1.0, base=0,
                                    pattern=[[-1, P]], channel_multiplier=1).then_inc(pool_consts, 1)
            nc.gpsimd.affine_select(out=before_me[:], in_=ones[:], compare_op=ALU.is_gt, fill=0.0, base=0,
                                    pattern=[[1, P]], channel_multiplier=-1).then_inc(pool_consts, 1)
            for dst, pattern, base, mult in ((tok_local[:], [[P, J]], 0, 1),
                                             (last_slot[:], [[-P, J]], SLOTS - 1, -1),
                                             (tok_value[:], [[-P, B * J]], N, -1),
                                             (tile_thr[:], [[-P, S0]], L, 0),
                                             (place_no[:], [[1, CAP]], 0, 0)):
                nc.gpsimd.iota(dst, pattern, base=base, channel_multiplier=mult,
                               allow_small_or_imprecise_dtypes=True).then_inc(pool_consts, 1)
            pool.dma_start(sorted_dram.rearrange("(s p) d -> p s d", p=P),
                           clear[:, 0:D].unsqueeze(1).broadcast_to([P, S0, D])).then_inc(scratch_clear, 16)
            pool.dma_start(table[N:ROWS, :], clear[0:CAP, :]).then_inc(scratch_clear, 16)
            pool.dma_start(out[N:ROWS, :], clear[0:CAP, 0:D]).then_inc(scratch_clear, 16)
            pool.wait_ge(x_loaded[0], 16)
            pool.wait_ge(w_attn_loaded, 16 * 5)
            pool.dma_start(odd_out.rearrange("(a p) d -> p a d", p=CAP),
                           clear[0:CAP, 0:D].unsqueeze(1).broadcast_to([CAP, ROWS // CAP, D])
                           ).then_inc(scratch_clear, 16)
            pool.wait_ge(scratch_clear, 64)

            def route_slots(b, _):
                wait_apart(pool, passed["pool"], (ln_steps[1], (b + 1) * LN), (route_steps, (b + 1) * RT),
                           (sorted_loaded, b * 16))
                for j in range(J):
                    pool.indirect_dma_start(sorted_dram, bass.IndirectOffsetOnAxis(slot_new[:, j:j + 1], 0),
                                            xn_f[:, j, :], None).then_inc(rows_sorted, 16)

            def ffn_out(b, _):
                wait_apart(pool, passed["pool"], (slot_kept, (b + 1) * 2), (ys_stored, (b + 1) * 16))
                for j in range(J):
                    pool.indirect_dma_start(xs[:, j, :], None, ysorted_dram,
                                            bass.IndirectOffsetOnAxis(slot_idx[:, j:j + 1], 0)).then_inc(yt_loaded, 16)

            def ssm_delta(b, c):
                pool.wait_ge(z_steps, (b * K + c + 1) * ZS)
                tt(sp_z[:, c, :], delta[:, c, :], y_fm[:, c, :], ALU.mult).then_inc(du_ready, 1)
                if c == 0:
                    pool.wait_ge(bc_loaded, (b + 1) * 16)
                    delta_b(b, 0)

            def ssm_skip(b, _):
                xn = xf[:, :, 0:D]
                tt(xn, xn, d_row[:].unsqueeze(1).broadcast_to([P, J, D]), ALU.mult).then_inc(skip_steps, 1)
                pool.wait_ge(skip_steps, b * 2 + 1)
                xb = x_res[:, bass.ds(b * J, J), :]
                tt(xb, xb, xn, ALU.add).then_inc(skip_steps, 1)

            def delta_b(b, g):
                c, n0 = g // (NS // GROUP), g % (NS // GROUP) * GROUP
                wait_from_one(pool, group_summed, b * GROUPS + max(g - 1, 0))
                pool.wait_ge(du_ready, b * K + c + 1)
                tt(hs[:, g % 2, :, :], sp_z[:, c, :].unsqueeze(1).broadcast_to([P, GROUP, L]), bc[:, n0:n0 + GROUP, :],
                   ALU.mult).then_inc(dbu_ready, 1)

            def ssm(b, g):
                if g + 1 < GROUPS:
                    delta_b(b, g + 1)
                if b not in C_ON_VECTOR:
                    pool.wait_ge(scanned, b * GROUPS + g + 1)
                    n0 = NS + g % (NS // GROUP) * GROUP
                    tt(hs[:, g % 2, :, :], hs[:, g % 2, :, :], bc[:, n0:n0 + GROUP, :], ALU.mult
                       ).then_inc(hc_ready, 1)

            def gates(b, _):
                wait_apart(pool, passed["pool"], (gate_steps, (b + 1) * GT))
                nc.gpsimd.tensor_copy(xf[:, :, D:XW], sc66[:, :, 0:E]).then_inc(scores_copied, 1)

            def fetch(p):
                pool.indirect_dma_start(xg[p % ROW_RING], None, table,
                                        bass.IndirectOffsetOnAxis(idx_get[:, p:p + 1], 0)
                                        ).then_inc(xg_loaded[p % ROW_RING], 16)

            def tables(b, _):
                pool.wait_ge(ids_steps, 6)
                pool.wait_ge(table_stored, 16 * B)
                for p in range(ROW_RING):
                    fetch(p)

            run(pool, dict(route_slots=route_slots, ffn_out=ffn_out, ssm_delta=ssm_delta, ssm=ssm, ssm_skip=ssm_skip, gates=gates,
                           tables=tables))

            pool.wait_ge(out_stored, 16 * B)
            for p in range(PAIRS):
                pool.wait_ge(yo_halves, 2 * (p + 1))
                for e in range(2):
                    wait_from_one(pool, rows_added[e], 16 * p)
                    pool.indirect_dma_start((out, odd_out)[e],
                                            bass.IndirectOffsetOnAxis(idx_add[:, 2 * p + e:2 * p + e + 1], 0),
                                            yo[e * CAP:(e + 1) * CAP, p % 2, :], None, compute_op=ALU.add
                                            ).then_inc(rows_added[e], 16)
                if p + ROW_RING < PAIRS:
                    fetch(p + ROW_RING)
            pool.wait_ge(rows_added[0], 16 * PAIRS)
            pool.wait_ge(rows_added[1], 16 * PAIRS)
            pool.dma_start(out[0:N, :].rearrange("(p r) d -> p (r d)", p=P),
                           odd_out[0:N, :].rearrange("(p r) d -> p (r d)", p=P), accum_op=ALU.add, max_dma_last_dim=8192
                           ).then_inc(sums_added, 16)

        @block.tensor
        def _(pe):
            turn, misc, gu, _ = rings()
            expert_of, gu_use, h_use = {}, {}, {}

            def transposes(blocks, *ready):
                slot, use = turn.next()
                wait_apart(pe, passed["pe"], (turn_moved, use - 1), *ready)
                for col, rows, width, src in blocks:
                    mm = pe.transpose(turn_ps[slot][0:width, col:col + rows], src, ident[0:rows, 0:rows])
                mm.then_inc(turn_filled, 1)

            def turn_tiles(src, tiles):
                for j0 in range(0, tiles, 2):
                    transposes([((jj * K + k) * P, P, P, src[:, j0 + jj, k * P:(k + 1) * P])
                                for jj in range(min(2, tiles - j0)) for k in range(K)])
                pe.wait_ge(turn_moved, turn.so_far())

            def attn_turn(b, _):
                if b == 0:
                    pe.wait_ge(pool_consts, 10)
                    pe.wait_ge(w_attn_loaded, 16 * 5)
                pe.wait_ge(ln_steps[0], (b + 1) * LN)
                turn_tiles(xn_f, J)

            def attn_qkv(b, _):
                for j in range(J):
                    _, use = misc.next()
                    wait_from_one(pe, misc_moved, use)
                    for k in range(K):
                        mm = pe.matmul(misc_ps[:, 0:QKV], xn_attn_t[:, k, j, :], w_qkv[:, k, :],
                                       start=(k == 0), stop=(k == K - 1))
                    mm.then_inc(misc_filled, 1)

            def route_slots(b, _):
                pe.wait_ge(route_steps, b * RT + RT_SEL)
                _, use = misc.next()
                wait_from_one(pe, misc_moved, use)
                pe.matmul(misc_ps[:, 0:J], before_me[:], rt[:, 6, 0:J], start=True, stop=True)
                pe.matmul(misc_ps[:, J:2 * J], ones[:], rt[:, 6, 0:J], start=True, stop=True).then_inc(misc_filled, 1)

            def ffn_in(b, _):
                if b == 0:
                    pe.wait_ge(w_ffn_loaded, 16 * 6)
                wait_apart(pe, passed["pe"], (route_steps, (b + 1) * RT))
                for j in range(S0):
                    expert_of[j] = pe.value_load(rt_ex[0:1, j:j + 1], min_val=0, max_val=1)
                pe.wait_ge(sorted_loaded, (b + 1) * 16)
                turn_tiles(xs, S0)

            def gate_up(b, s):
                j, half = s // HALF, s % HALF
                slot, use = gu.next()
                gu_use[s] = use
                wait_from_one(pe, gu_used, gu.free_at)
                for g, bank in ((0, gate_ps[slot]), (1, up_ps[slot])):
                    for k in range(K):
                        mm = pe.matmul(bank[:], xs_t[:, k, j, :],
                                       gu0[:, expert_of[j], k, g, half * 512:(half + 1) * 512],
                                       start=(k == 0), stop=(k == K - 1))
                mm.then_inc(gu_filled, 1)

            def turn_h(b, s):
                pe.wait_ge(gu_used, gu_use[s] + 1)
                h_use[s] = turn.so_far()
                transposes([(c * P, P, P, h0[:, s % 2, c * P:(c + 1) * P]) for c in range(4)])

            def down(b, s):
                j, half = s // HALF, s % HALF
                pe.wait_ge(turn_moved, h_use[s] + 1)
                if half == 0:
                    wait_from_one(pe, down_moved, b * S0 + j)
                for c in range(4):
                    mm = pe.matmul(down_ps[:, 0:D], h0_t[:, s % 2, c * P:(c + 1) * P],
                                   dn0[:, expert_of[j], half * 4 + c, :],
                                   start=(half == 0 and c == 0), stop=(half == 1 and c == 3))
                if half == 1:
                    mm.then_inc(down_filled, 1)

            def ffn(b, s):
                gate_up(b, s)
                if s >= 1:
                    turn_h(b, s - 1)
                if s >= 2:
                    down(b, s - 2)

            def ffn_tail(b, _):
                turn_h(b, STEPS - 1)
                down(b, STEPS - 2)
                down(b, STEPS - 1)

            def ssm_in(b, _):
                pe.wait_ge(w_ssm_loaded, 16 * 5)
                pe.wait_ge(ln_steps[2], (b + 1) * LN)
                turn_tiles(xf, J)

            def ssm_proj(b, _):
                _, use = misc.next()
                pe.wait_ge(misc_moved, use)
                for k in range(K):
                    mm = pe.matmul(misc_ps[0:R + 2 * NS, :], w_x[:, k, :], y_fm[:, k, :],
                                   start=(k == 0), stop=(k == K - 1))
                mm.then_inc(misc_filled, 1)
                for c in range(K):
                    _, use = misc.next()
                    pe.wait_ge(misc_moved, use)
                    pe.matmul(misc_ps[:], w_dt[:, c * P:(c + 1) * P], x_dbl[0:R, :], start=True, stop=True
                              ).then_inc(misc_filled, 1)

            def ssm_out(b, _):
                pe.wait_ge(group_summed, (b + 1) * GROUPS)
                for j0 in range(0, J, 2):
                    transposes([((jj * K + c) * P, P, P, y_fm[:, c, (j0 + jj) * P:(j0 + jj + 1) * P])
                                for jj in range(2) for c in range(K)])

            def gates_in(b, _):
                pe.wait_ge(w_tail_loaded, 16 * 5)
                pe.wait_ge(ln_steps[3], (b + 1) * LN)
                turn_tiles(xf, J)

            def gates(b, _):
                _, use = misc.next()
                pe.wait_ge(misc_moved, use)
                for j in range(J):
                    for k in range(K):
                        mm = pe.matmul(misc_ps[:, j * E:(j + 1) * E], back_t[:, k, j, :], w_g1[:, k, :],
                                       start=(k == 0), stop=(k == K - 1))
                mm.then_inc(misc_filled, 1)

            def places(b, _):
                transposes([(j * P, P, E, marked[:, j, 0:E]) for j in range(J)], (top_steps, (b + 1) * TOP))

            def shared(b, m):
                rows = SH_ROWS[m]
                slot, use = gu.next(2 if m == 2 else 1)
                pe.wait_ge(gu_used, gu.free_at)
                for g, bank in ((0, gate_ps[slot]), (1, up_ps[slot])):
                    for k in range(K):
                        mm = pe.matmul(bank[0:rows, :], w_sh[:, k, g, m * P:m * P + rows], y_fm[:, k, :],
                                       start=(k == 0), stop=(k == K - 1))
                    if g == 1 or m == 2:
                        mm.then_inc(gu_filled, 1)

            def shared_out(b, _):
                pe.wait_ge(gu_used, gu.so_far())
                for j0 in range(0, J, 2):
                    _, use = misc.next()
                    pe.wait_ge(misc_moved, use)
                    for jj in range(2):
                        for m, rows in enumerate(SH_ROWS):
                            mm = pe.matmul(misc_ps[:, jj * D:(jj + 1) * D],
                                           hsh_t[0:rows, m, (j0 + jj) * P:(j0 + jj + 1) * P],
                                           w_shd[0:rows, m, :], start=(m == 0), stop=(m == 2))
                    mm.then_inc(misc_filled, 1)

            def tables(b, _):
                pe.wait_ge(ids_steps, 3)
                transposes([(0, CAP, P, ids[:].rearrange("e a s -> e (a s)"))])
                pe.wait_ge(turn_moved, turn.so_far())

            run(pe, dict(attn_turn=attn_turn, attn_qkv=attn_qkv, route_slots=route_slots, ffn_in=ffn_in, ffn=ffn,
                         ffn_tail=ffn_tail, ssm_in=ssm_in, ssm_proj=ssm_proj, ssm_out=ssm_out, gates_in=gates_in,
                         gates=gates, places=places, shared=shared, shared_out=shared_out, tables=tables))

            def turn_rows(p, slot, count):
                pe.wait_ge(xg_loaded[slot], 16 * count)
                wait_from_one(pe, xgt_ready, p)
                for k in range(K):
                    mm = pe.transpose(turn_ps[0][:, k * P:(k + 1) * P], xg[slot][:, k * P:(k + 1) * P], ident[:])
                mm.then_inc(xg_turned, 1)

            def gate_up1(p, q, i):
                pe.wait_ge(pair_loaded[q % RING], 48 * (i * (ROW_RING // RING) + q // RING + 1))
                pe.wait_ge(xgt_ready, p + 1)
                wait_from_one(pe, h1_ready, p - 1)
                for k in range(K):
                    for e in range(2):
                        mm = pe.matmul(gate_ps[q % 2][e * CAP:(e + 1) * CAP, 0:FSH],
                                       xg_t[:, q % 2, k, e * CAP:(e + 1) * CAP], gu1[q % RING][:, e * K + k, :],
                                       start=(k == 0), stop=(k == K - 1))
                mm.then_inc(gu1_filled, 1)

            def turn_h1(p, par):
                pe.wait_ge(h1_ready, p + 1)
                wait_from_one(pe, h1t_ready, p)
                for c in range(2):
                    mm = pe.transpose(turn_ps[1][0:FC, c * P:(c + 1) * P], h1[:, par, c * FC:(c + 1) * FC], ident[:])
                mm.then_inc(h1_turned, 1)

            def down1(p, slot):
                par = slot % 2
                pe.wait_ge(h1t_ready, p + 1)
                wait_from_one(pe, yo_halves, 2 * (p - 1))
                for c in range(2):
                    for e in range(2):
                        mm = pe.matmul(y_ps[par][e * CAP:(e + 1) * CAP, 0:D],
                                       h1_t[:, par, c, e * CAP:(e + 1) * CAP], dn1[slot % RING][:, e * 2 + c, :],
                                       start=(c == 0), stop=(c == 1))
                mm.then_inc(down1_filled, 1)

            def pair(p, q, i):
                gate_up1(p, q, i)
                if not isinstance(p, int) or p + 1 < PAIRS:
                    turn_rows(p + 1, (q + 1) % ROW_RING, i + 1 if q + 1 < ROW_RING else i + 2)
                if not isinstance(p, int) or p >= 1:
                    turn_h1(p - 1, (q - 1) % 2)
                if not isinstance(p, int) or p >= 2:
                    down1(p - 2, (q - 2) % ROW_RING)

            turn_rows(0, 0, 1)
            run_pairs(pe, pair)
            turn_h1(PAIRS - 1, (PAIRS - 1) % 2)
            down1(PAIRS - 2, (PAIRS - 2) % ROW_RING)
            down1(PAIRS - 1, (PAIRS - 1) % ROW_RING)

        @block.scalar
        def _(act):
            act.preload_act_table_set("exp_and_others")
            turn, misc, gu, _ = rings()

            def move_turned(out_ap, of_bank):
                slot, use = turn.next()
                act.wait_ge(turn_filled, use + 1)
                nc.scalar.copy(out_ap, of_bank(turn_ps[slot])).then_inc(turn_moved, 1)

            def move_tiles(dst, tiles):
                for j0 in range(0, tiles, 2):
                    w = min(2, tiles - j0)
                    move_turned(dst[:, :, j0:j0 + w, :],
                                lambda bank: bank[:, 0:w * K * P].rearrange("p (j k t) -> p k j t", j=w, k=K))

            def attn_turn(b, _):
                move_tiles(xn_attn_t, J)

            def attn_score(b, _):
                act.wait_ge(attn_steps, b * AT + AT_DIFF)
                nc.scalar.activation(att_s[:, 3, :], att_s[:, 2, :], ACT.Exp, scale=HD ** -0.5).then_inc(attn_exp, 1)

            def route_gate(b, _):
                act.wait_ge(route_steps, b * RT + RT_DIFF)
                nc.scalar.activation(rt[:, 3, :], rt[:, 2, :], ACT.Exp).then_inc(route_exp, 1)

            def ffn_in(b, _):
                move_tiles(xs_t, S0)

            def half_tanh(rows, uses):
                slot, use = gu.next(uses)
                act.wait_ge(gu_filled, use + uses)
                wait_from_one(act, gu_used, gu.free_at)
                nc.scalar.activation(sig[0:rows, slot, :], gate_ps[slot][0:rows, :], ACT.Tanh, scale=0.5
                                     ).then_inc(tanh_ready, 1)

            def move_h(s):
                move_turned(h0_t[:, s % 2, :], lambda bank: bank[:])

            def move_y(b, j):
                act.wait_ge(down_filled, b * S0 + j + 1)
                nc.scalar.copy(xs[:, j, :], down_ps[:, 0:D]).then_inc(down_moved, 1)

            def ffn(b, s):
                half_tanh(P, 1)
                if s >= 1:
                    move_h(s - 1)
                if s >= 3 and (s - 2) % HALF == 1:
                    move_y(b, (s - 2) // HALF)

            def ffn_tail(b, _):
                move_h(STEPS - 1)
                move_y(b, S0 - 1)

            def ssm_in(b, _):
                if b == 0:
                    act.wait_ge(w_ssm_loaded, 16 * 5)
                    nc.scalar.activation(a_col[:], a_col[:], ACT.Exp).then_inc(a_ready, 1)
                move_tiles(back_t, J)

            def ssm_proj(b, _):
                _, use = misc.next(1 + K)
                act.wait_ge(misc_filled, use + 1)
                wait_from_one(act, bc_stored, b * 16)
                nc.scalar.copy(x_dbl[:], misc_ps[0:R + 2 * NS, :]).then_inc(misc_moved, 1)

            def ssm_exp(b, _):
                act.wait_ge(z_ready, (b + 1) * K)
                nc.scalar.activation(sp_e, sp_z[:], ACT.Abs).then_inc(sp_funcs, 1)
                act.wait_ge(sp_funcs, b * 2 + 1)
                nc.scalar.activation(sp_e, sp_e, ACT.Exp, scale=-1.0).then_inc(sp_funcs, 1)

            def ssm(b, g):
                c, n0 = g // (NS // GROUP), g % (NS // GROUP) * GROUP
                if n0 == 0:
                    act.wait_ge(z_steps, (b * K + c + 1) * ZS)
                if g == 0:
                    act.wait_ge(a_ready, 2)
                    act.wait_ge(dve_consts, 1)
                wait_from_one(act, scanned, b * GROUPS + max(g - 1, 0))
                for n in range(GROUP):
                    nc.scalar.activation(d_a[:, g % 2, n, 1:L], delta[:, c, 1:L], ACT.Exp,
                                         scale=a_col[:, c, n0 + n:n0 + n + 1]).then_inc(da_ready, 1)

            def ssm_out(b, _):
                wait_from_one(act, out_stored, b * 16)
                for j0 in range(0, J, 2):
                    move_turned(y_tok[:, j0:j0 + 2, :], lambda bank: bank[:].rearrange("p (j d) -> p j d", j=2))

            def gates_in(b, _):
                move_tiles(back_t, J)

            def gates(b, _):
                _, use = misc.next()
                act.wait_ge(misc_moved, use + 1)
                nc.scalar.activation(sc[:], sc[:], ACT.Exp).then_inc(gate_exp, 1)

            def places(b, _):
                wait_from_one(act, round_steps, b * RD)
                act.wait_ge(dve_consts, 4)
                move_turned(work[:, CAP:CAP + L], lambda bank: bank[0:E, :])

            def shared(b, m):
                half_tanh(SH_ROWS[m], 2 if m == 2 else 1)

            def tables(b, _):
                move_turned(ids_t, lambda bank: bank[:, 0:E])

            run(act, dict(attn_turn=attn_turn, attn_score=attn_score, route_gate=route_gate, ffn_in=ffn_in, ffn=ffn,
                          ffn_tail=ffn_tail, ssm_in=ssm_in, ssm_proj=ssm_proj, ssm_exp=ssm_exp, ssm=ssm,
                          ssm_out=ssm_out, gates_in=gates_in, gates=gates, places=places, shared=shared,
                          tables=tables),
                [(misc, MISCS, ("ssm_proj", "gates"))])

            def move_rows(p, par):
                act.wait_ge(xg_turned, p + 1)
                nc.scalar.copy(xg_t[:, par, :, :], turn_ps[0][:, 0:K * P].rearrange("p (k t) -> p k t", k=K)
                               ).then_inc(xgt_ready, 1)

            def move_h1(p, par):
                act.wait_ge(h1_turned, p + 1)
                nc.scalar.copy(h1_t[:, par, :, :], turn_ps[1][0:FC, 0:2 * P].rearrange("p (c t) -> p c t", c=2)
                               ).then_inc(h1t_ready, 1)

            def pair(p, q, i):
                act.wait_ge(gu1_filled, p + 1)
                wait_from_one(act, h1_ready, p - 1)
                nc.scalar.activation(sig1[:, q % 2, :], gate_ps[q % 2][:, 0:F1], ACT.Tanh, scale=0.5
                                     ).then_inc(tanh1_ready, 1)
                if not isinstance(p, int) or p + 1 < PAIRS:
                    move_rows(p + 1, (q + 1) % 2)
                if not isinstance(p, int) or p >= 1:
                    move_h1(p - 1, (q - 1) % 2)

            move_rows(0, 0)
            run_pairs(act, pair)
            move_h1(PAIRS - 1, (PAIRS - 1) % 2)

        @block.vector
        def _(dve):
            turn, misc, gu, silu_ring = rings()
            tt, ts, stt = nc.vector.tensor_tensor, nc.vector.tensor_scalar, nc.vector.scalar_tensor_tensor
            reduce, recip = nc.vector.tensor_reduce, nc.vector.reciprocal

            def wide(ap, n):
                return ap.unsqueeze(2).broadcast_to([P, ap.shape[1], n])

            def norm(n, b, dst):
                s, w, mv = ln_steps[n], ln_w[n], ln_mv[n]
                for j in range(J):
                    nc.vector.bn_stats(ln_st[n][:, j, :], x_res[:, b * J + j, :]).then_inc(s, 1)
                wait_apart(dve, passed["dve"], (s, b * LN + J))
                for j in range(J):
                    nc.vector.bn_aggr(mv[:, j, :], ln_st[n][:, j, :]).then_inc(s, 1)
                dve.wait_ge(s, b * LN + 2 * J)
                ts(w[:, 0, :], mv[:, :, 1], EPS, None, ALU.add).then_inc(s, 1)
                dve.wait_ge(s, b * LN + 2 * J + 1)
                v, t, r = (w[:, row, :] for row in range(3))
                ts(t.bitcast(I32), v.bitcast(I32), 1, None, ALU.logical_shift_right).then_inc(s, 1)
                dve.wait_ge(s, b * LN + 2 * J + 2)
                ts(r.bitcast(I32), t.bitcast(I32), -1.0, float(HALF_EXPONENT), ALU.mult, ALU.add).then_inc(s, 1)
                for step in range(NEWTON):
                    dve.wait_ge(s, b * LN + 2 * J + 3 + 3 * step)
                    tt(t, r, r, ALU.mult).then_inc(s, 1)
                    dve.wait_ge(s, b * LN + 2 * J + 4 + 3 * step)
                    stt(out=t, in0=t, scalar=-0.5, in1=v, op0=ALU.mult, op1=ALU.mult).then_inc(s, 1)
                    dve.wait_ge(s, b * LN + 2 * J + 5 + 3 * step)
                    stt(out=r, in0=t, scalar=1.5, in1=r, op0=ALU.add, op1=ALU.mult).then_inc(s, 1)
                dve.wait_ge(s, b * LN + 2 * J + 3 + 3 * NEWTON)
                for j in range(J):
                    ts(dst[:, j, 0:D], x_res[:, b * J + j, :], mv[:, j, 0:1], r[:, j:j + 1],
                       ALU.subtract, ALU.mult).then_inc(s, 1)

            def attn_in(b, _):
                if b == 0:
                    dve.wait_ge(x_loaded[0], 16)
                    dve.wait_ge(pool_consts, 10)
                elif b == 1:
                    for loaded in x_loaded[1:]:
                        dve.wait_ge(loaded, 16)
                wait_from_one(dve, rows_sorted, b * 16 * J)
                norm(0, b, xn_f)

            def attn_qkv(b, _):
                if b == 0:
                    dve.wait_ge(w_attn_loaded, 16 * 5)
                wait_from_one(dve, out_stored, (b - 2) * 16)
                for j in range(J):
                    _, use = misc.next()
                    dve.wait_ge(misc_filled, use + 1)
                    tt(q_buf[:, j, :], misc_ps[:, 0:D], b_qkv[:, 0:D], ALU.add).then_inc(attn_steps, 1)
                    tt(kv[:, j, :], misc_ps[:, D:QKV], b_qkv[:, D:QKV], ALU.add).then_inc(misc_moved, 1)
                dve.wait_ge(misc_moved, use + 1)

            w4 = mix.rearrange("p j (h d) -> p j h d", h=H)
            score, best, diff, ex, den, rec, prob = (att_s[:, r, :] for r in range(7))

            def attn_score(b, _):
                dve.wait_ge(attn_steps, b * AT + J)
                q4 = q_buf.rearrange("p j (h d) -> p j h d", h=H)
                k4 = kv[:, :, 0:HD].unsqueeze(2).broadcast_to([P, J, H, HD])
                tt(w4, q4, k4, ALU.mult).then_inc(attn_steps, 1)
                dve.wait_ge(attn_steps, b * AT + J + 1)
                reduce(score, mix.rearrange("p j (h d) -> p (j h) d", h=H), AX, ALU.add).then_inc(attn_steps, 1)
                dve.wait_ge(attn_steps, b * AT + J + 2)
                reduce(best, score.unsqueeze(2), AX, ALU.max).then_inc(attn_steps, 1)
                dve.wait_ge(attn_steps, b * AT + J + 3)
                tt(diff, score, best, ALU.subtract).then_inc(attn_steps, 1)

            def attn_add(b, _):
                v4 = kv[:, :, HD:2 * HD].unsqueeze(2).broadcast_to([P, J, H, HD])
                dve.wait_ge(attn_exp, b + 1)
                reduce(den, ex.unsqueeze(2), AX, ALU.add).then_inc(attn_steps, 1)
                dve.wait_ge(attn_steps, b * AT + J + 5)
                recip(rec, den).then_inc(attn_steps, 1)
                dve.wait_ge(attn_steps, b * AT + J + 6)
                tt(prob, ex, rec, ALU.mult).then_inc(attn_steps, 1)
                dve.wait_ge(attn_steps, b * AT + J + 7)
                tt(w4, v4, prob.rearrange("p (j h) -> p j h", j=J).unsqueeze(3).broadcast_to([P, J, H, HD]),
                   ALU.mult).then_inc(attn_steps, 1)
                dve.wait_ge(attn_steps, b * AT + J + 8)
                xb = x_res[:, bass.ds(b * J, J), :]
                tt(xb, xb, mix, ALU.add).then_inc(attn_steps, 1)
                wait_apart(dve, passed["dve"], (attn_steps, (b + 1) * AT))

            def route_gate(b, _):
                norm(1, b, xn_f)
                dve.wait_ge(ln_steps[1], (b + 1) * LN)
                s = route_steps
                for j in range(J):
                    for e in range(2):
                        nc.vector.tensor_tensor_reduce(out=(mix[:, j, :], xn_t[:, j * D:(j + 1) * D])[e], in0=xn_f[:, j, :], in1=g0_row[:, e, :],
                                                       scale=1.0, scalar=0.0, op0=ALU.mult, op1=ALU.add,
                                                       accum_out=rt[:, 0, 2 * j + e:2 * j + e + 1]).then_inc(s, 1)
                dve.wait_ge(s, b * RT + 8)
                lg = rt[:, 0, :].rearrange("p (j e) -> p j e", e=2)
                best = rt[:, 1, 0:J]
                reduce(best, lg, AX, ALU.max).then_inc(s, 1)
                tt(rt[:, 6, 0:J], lg[:, :, 1], lg[:, :, 0], ALU.is_gt).then_inc(s, 1)
                dve.wait_ge(s, b * RT + 9)
                tt(rt[:, 2, :].rearrange("p (j e) -> p j e", e=2), lg, wide(best, 2), ALU.subtract).then_inc(s, 1)

            def route_slots(b, _):
                s = route_steps
                dve.wait_ge(route_exp, b + 1)
                ex = rt[:, 3, :].rearrange("p (j e) -> p j e", e=2)
                reduce(rt[:, 4, 0:J], ex, AX, ALU.add).then_inc(s, 1)
                reduce(rt[:, 4, J:2 * J], ex, AX, ALU.max).then_inc(s, 1)
                dve.wait_ge(s, b * RT + 13)
                recip(rt[:, 5, 0:J], rt[:, 4, 0:J]).then_inc(s, 1)
                dve.wait_ge(s, b * RT + 14)
                tt(rt[:, 5, J:2 * J], rt[:, 4, J:2 * J], rt[:, 5, 0:J], ALU.mult).then_inc(s, 1)
                _, use = misc.next()
                dve.wait_ge(misc_filled, use + 1)
                nc.vector.tensor_copy(rt[:, 7, :], misc_ps[:, 0:2 * J]).then_inc(misc_moved, 1)
                dve.wait_ge(misc_moved, use + 1)
                nc.vector.tensor_tensor_scan(rt[:, 8, 0:J], ones[:, 0:J], rt[:, 7, J:2 * J], 0.0,
                                             ALU.mult, ALU.add).then_inc(s, 1)
                tt(rt[:, 9, 0:J], rt[:, 7, 0:J], rt[:, 7, J:2 * J], ALU.subtract).then_inc(s, 1)
                tt(rt[:, 10, 0:J], rt[:, 6, 0:J], last_slot[:], ALU.mult).then_inc(s, 1)
                dve.wait_ge(s, b * RT + 18)
                tt(rt[:, 11, 0:J], rt[:, 9, 0:J], rt[:, 8, 0:J], ALU.add).then_inc(s, 1)
                dve.wait_ge(s, b * RT + 19)
                tt(rt[:, 12, 0:J], tok_local[:], rt[:, 11, 0:J], ALU.subtract).then_inc(s, 1)
                dve.wait_ge(s, b * RT + 20)
                tt(slot_new[:], rt[:, 12, 0:J], rt[:, 10, 0:J], ALU.add).then_inc(s, 1)
                ts(rt_ex[:], tile_thr[:], rt[0:1, 8, J - 1:J], None, ALU.is_le).then_inc(s, 1)

            def silu(rows, dst, uses):
                slot, use = gu.next(uses)
                _, n = silu_ring.next()
                dve.wait_ge(tanh_ready, n + 1)
                s = sig[0:rows, slot, :]
                stt(out=s, in0=s, scalar=1.0, in1=gate_ps[slot][0:rows, :], op0=ALU.add, op1=ALU.mult
                    ).then_inc(silu_steps, 1)
                dve.wait_ge(silu_steps, n + 1)
                w = 512 // uses
                for u in range(0, 512, w):
                    stt(out=dst[:, u:u + w], in0=s[:, u:u + w], scalar=0.5, in1=up_ps[slot][0:rows, u:u + w],
                        op0=ALU.mult, op1=ALU.mult).then_inc(gu_used, 1)

            def ffn_in(b, _):
                wait_from_one(dve, yt_loaded, b * 16 * J)
                dve.wait_ge(route_steps, (b + 1) * RT)
                nc.vector.tensor_copy(slot_idx[:], slot_new[:]).then_inc(slot_kept, 1)
                nc.vector.tensor_copy(slot_w[:], rt[:, 5, J:2 * J]).then_inc(slot_kept, 1)

            def ffn(b, s):
                silu(P, h0[:, s % 2, :], 1)

            def ffn_out(b, _):
                dve.wait_ge(yt_loaded, (b + 1) * 16 * J)
                dve.wait_ge(slot_kept, (b + 1) * 2)
                for j in range(J):
                    xt = x_res[:, b * J + j, :]
                    stt(out=xt, in0=xs[:, j, :], scalar=slot_w[:, j:j + 1], in1=xt,
                        op0=ALU.mult, op1=ALU.add).then_inc(x_after_ffn, 1)
                wait_apart(dve, passed["dve"], (x_after_ffn, (b + 1) * J))

            def ssm_norm(b, _):
                wait_apart(dve, passed["dve"], (table_stored, b * 16))
                norm(2, b, xf)

            def ssm_proj(b, _):
                if b == 0:
                    dve.wait_ge(a_ready, 1)
                    ts(a_col[:], a_col[:], -1.0, None, ALU.mult).then_inc(a_ready, 1)
                misc.next()
                for c in range(K):
                    _, use = misc.next()
                    dve.wait_ge(misc_filled, use + 1)
                    ts(sp_z[:, c, :], misc_ps[:], bdt_col[:, c:c + 1], None, ALU.add).then_inc(misc_moved, 1)
                dve.wait_ge(misc_moved, use + 1)
                dve.sem_inc(z_ready, K)

            def ssm_delta(b, c):
                s, done = z_steps, (b * K + c) * ZS
                e, d = sp_e[:, c, :], delta[:, c, :]
                dve.wait_ge(sp_funcs, b * 2 + 2)
                ts(d, e, LOG1P[-1], None, ALU.mult).then_inc(s, 1)
                for k in range(len(LOG1P) - 2, -1, -1):
                    dve.wait_ge(s, done + len(LOG1P) - 1 - k)
                    stt(out=d, in0=d, scalar=LOG1P[k], in1=e, op0=ALU.add, op1=ALU.mult).then_inc(s, 1)
                dve.wait_ge(s, done + len(LOG1P))
                stt(out=d, in0=sp_z[:, c, :], scalar=0.0, in1=d, op0=ALU.max, op1=ALU.add).then_inc(s, 1)

            def ssm(b, g):
                flat = "p n l -> p (n l)"
                buf = hs[:, g % 2, :, :]
                dve.wait_ge(da_ready, b * GROUPS * GROUP + GROUP * g + GROUP)
                dve.wait_ge(dbu_ready, b * GROUPS + g + 1)
                nc.vector.tensor_tensor_scan(buf.rearrange(flat), d_a[:, g % 2, :, :].rearrange(flat),
                                             buf.rearrange(flat), 0.0, ALU.mult, ALU.add).then_inc(scanned, 1)
                if b in C_ON_VECTOR:
                    n0 = NS + g % (NS // GROUP) * GROUP
                    dve.wait_ge(scanned, b * GROUPS + g + 1)
                    tt(buf, buf, bc[:, n0:n0 + GROUP, :], ALU.mult).then_inc(hc_ready, 1)
                    add_up(b, g)
                elif g >= 1:
                    add_up(b, g - 1)

            def add_up(b, g):
                c, quarter = g // (NS // GROUP), g % (NS // GROUP)
                dve.wait_ge(hc_ready, b * GROUPS + g + 1)
                if quarter == 0:
                    tt(y_fm[:, c, :], hs[:, g % 2, 0, :], hs[:, g % 2, 1, :], ALU.add).then_inc(group_summed, 1)
                else:
                    dve.wait_ge(group_summed, b * GROUPS + g)
                    tt(y_half[:], hs[:, g % 2, 0, :], hs[:, g % 2, 1, :], ALU.add).then_inc(sum_steps, 1)
                    dve.wait_ge(sum_steps, b * (GROUPS - K) + g - c)
                    tt(y_fm[:, c, :], y_fm[:, c, :], y_half[:], ALU.add).then_inc(group_summed, 1)

            def ssm_skip(b, _):
                if b not in C_ON_VECTOR:
                    add_up(b, GROUPS - 1)

            def ssm_out(b, _):
                _, use = turn.next(2)
                dve.wait_ge(turn_moved, use + 2)
                dve.wait_ge(skip_steps, (b + 1) * 2)
                xb = x_res[:, bass.ds(b * J, J), :]
                tt(xb, xb, y_tok, ALU.add).then_inc(x_after_ssm, 1)
                wait_apart(dve, passed["dve"], (x_after_ssm, b + 1))

            def gates_in(b, _):
                norm(3, b, xf)

            def gates(b, _):
                _, use = misc.next()
                s = gate_steps
                dve.wait_ge(misc_filled, use + 1)
                lg = misc_ps[:, 0:J * E].rearrange("p (j e) -> p j e", j=J)
                reduce(sc_s[:, 0, :], lg, AX, ALU.max).then_inc(s, 1)
                dve.wait_ge(s, b * GT + 1)
                tt(sc[:], lg, wide(sc_s[:, 0, :], E), ALU.subtract).then_inc(misc_moved, 1)
                dve.wait_ge(gate_exp, b + 1)
                reduce(sc_s[:, 1, :], sc[:], AX, ALU.add).then_inc(s, 1)
                dve.wait_ge(s, b * GT + 2)
                recip(sc_s[:, 2, :], sc_s[:, 1, :]).then_inc(s, 1)
                dve.wait_ge(s, b * GT + 3)
                wait_from_one(dve, scores_copied, b)
                tt(sc66[:, :, 0:E], sc[:], wide(sc_s[:, 2, :], E), ALU.mult).then_inc(s, 1)
                wait_apart(dve, passed["dve"], (s, (b + 1) * GT))

            def places(b, _):
                values_turned[b] = turn.so_far()
                s = top_steps
                dve.wait_ge(dve_consts, 4)
                for j in range(J):
                    nc.vector.max(top[:, j, :], sc66[:, j, :]).then_inc(s, 1)
                dve.wait_ge(s, b * TOP + J)
                nc.vector.memset(top[:, :, TOPK:TOPK + 1], -1.0).then_inc(s, 1)
                nc.vector.memset(top[:, :, TOPK + 1:TOPK + 2], -2.0).then_inc(s, 1)
                wait_apart(dve, passed["dve"], (s, b * TOP + J + 2))
                for j in range(J):
                    nc.vector.match_replace(out=marked[:, j, :], in_to_replace=top[:, j, :], in_values=sc66[:, j, :],
                                            imm_value=-3.0).then_inc(s, 1)
                dve.wait_ge(s, b * TOP + 2 * J + 2)
                stt(out=marked[:, :, 0:E], in0=marked[:, :, 0:E], scalar=-3.0,
                    in1=wide(tok_value[:, bass.ds(b * J, J)], E), op0=ALU.is_equal, op1=ALU.mult).then_inc(s, 1)

            values_turned = {}

            def rounds(b, m):
                s = round_steps
                if m == 0:
                    dve.wait_ge(turn_moved, values_turned[b])
                first, last = m * ROUNDS // 3, (m + 1) * ROUNDS // 3
                for r in range(first, last):
                    nc.vector.max(keep[:, 8 * r:8 * r + 8], work[:]).then_inc(s, 1)
                    dve.wait_ge(s, b * RD + 2 * r + 1)
                    nc.vector.match_replace(out=work[:], in_to_replace=keep[:, 8 * r:8 * r + 8], in_values=work[:],
                                            imm_value=0.0).then_inc(s, 1)
                    dve.wait_ge(s, b * RD + 2 * r + 2)
                if last == ROUNDS:
                    nc.vector.tensor_copy(work[:, 0:CAP], keep[:]).then_inc(s, 1)
                    dve.wait_ge(s, (b + 1) * RD)

            def shared(b, m):
                silu(SH_ROWS[m], hsh_t[0:SH_ROWS[m], m, :], 2 if m == 2 else 1)

            def shared_out(b, _):
                for j0 in range(0, J, 2):
                    _, use = misc.next()
                    dve.wait_ge(misc_filled, use + 1)
                    tt(o_sb[:, j0:j0 + 2, :], x_res[:, bass.ds(b * J + j0, 2), :],
                       misc_ps[:].rearrange("p (j d) -> p j d", j=2), ALU.add).then_inc(misc_moved, 1)

            nc.vector.memset(d_a[:], 0.0).then_inc(dve_consts, 1)
            nc.vector.memset(work[:], 0.0).then_inc(dve_consts, 1)
            nc.vector.memset(sc66[:, :, E:E + 1], -1.0).then_inc(dve_consts, 1)
            nc.vector.memset(sc66[:, :, E + 1:E + 2], -2.0).then_inc(dve_consts, 1)
            def tables(b, _):
                stt(out=ids_z[:], in0=keep[:], scalar=0.0, in1=place_no[:], op0=ALU.is_equal, op1=ALU.mult
                    ).then_inc(ids_steps, 1)
                dve.wait_ge(ids_steps, 1)
                for half in range(2):
                    stt(out=ids[:, half, :], in0=ids_z[:], scalar=float(N), in1=keep[:], op0=ALU.add, op1=ALU.subtract
                        ).then_inc(ids_steps, 1)
                turn.next()
                dve.wait_ge(turn_moved, turn.so_far())
                by_pair = ids_t.rearrange("p (n e) -> p n e", e=2)
                for e in range(2):
                    rows = slice(e * CAP, (e + 1) * CAP)
                    nc.vector.tensor_copy(idx_get[rows, :], by_pair[rows, :, e]).then_inc(ids_steps, 1)
                nc.vector.tensor_copy(idx_add[:], ids_t[0:CAP, :]).then_inc(ids_steps, 1)

            run(dve, dict(attn_in=attn_in, attn_qkv=attn_qkv, attn_score=attn_score, attn_add=attn_add,
                          route_gate=route_gate, route_slots=route_slots, ffn_in=ffn_in, ffn=ffn, ffn_out=ffn_out,
                          ssm_norm=ssm_norm, ssm_proj=ssm_proj, ssm_delta=ssm_delta, ssm=ssm, ssm_skip=ssm_skip,
                          ssm_out=ssm_out, gates_in=gates_in, gates=gates, places=places, shared=shared,
                          shared_out=shared_out, rounds=rounds, tables=tables),
                [(turn, TURNS, ("ssm_out", "tables"))])

            def weigh(p, slot):
                par = slot % 2
                dve.wait_ge(down1_filled, p + 1)
                for added in rows_added:
                    wait_from_one(dve, added, 16 * (p - 1))
                for e in range(2):
                    rows = slice(e * CAP, (e + 1) * CAP)
                    col = D + e + 2 * p
                    ts(yo[rows, par, :], y_ps[par][rows, 0:D], xg[slot][rows, bass.ds(col, 1)], None,
                       ALU.mult).then_inc(yo_halves, 1)

            def pair(p, q, i):
                par = q % 2
                s = sig1[:, par, :]
                dve.wait_ge(tanh1_ready, p + 1)
                stt(out=s, in0=s, scalar=1.0, in1=gate_ps[par][:, 0:F1], op0=ALU.add, op1=ALU.mult
                    ).then_inc(silu1_steps, 1)
                dve.wait_ge(silu1_steps, p + 1)
                stt(out=h1[:, par, :], in0=s, scalar=0.5, in1=gate_ps[par][:, F1:FSH], op0=ALU.mult, op1=ALU.mult
                    ).then_inc(h1_ready, 1)
                if not isinstance(p, int) or p >= 2:
                    weigh(p - 2, (q - 2) % ROW_RING)

            run_pairs(dve, pair)
            weigh(PAIRS - 2, (PAIRS - 2) % ROW_RING)
            weigh(PAIRS - 1, (PAIRS - 1) % ROW_RING)


def kernel(**inputs):
    import numpy as np
    import concourse.bacc as bacc
    from concourse.bass_utils import run_bass_kernel_spmd

    def arr(name, *axes):
        a = np.asarray(inputs[name])
        return np.ascontiguousarray(a.transpose(axes) if axes else a)

    arrays = {
        "x": arr("L0_attn_x").reshape(N, D),
        "wq_t": arr("L0_attn_Wq", 1, 0), "bq": arr("L0_attn_bq"),
        "wkv_t": arr("L0_attn_Wkv", 1, 0), "bkv": arr("L0_attn_bkv"),
        "gate0": arr("L0_ffn_gate_w"),
        "wg0_t": arr("L0_ffn_w_gate", 0, 2, 1), "wu0_t": arr("L0_ffn_w_up", 0, 2, 1),
        "wd0_t": arr("L0_ffn_w_down", 0, 2, 1),
        "wx_t": arr("L1_attn_W_xproj", 1, 0), "wdt_t": arr("L1_attn_W_dt", 1, 0),
        "b_dt": np.ascontiguousarray(arr("L1_attn_b_dt").reshape(K, P).T), "a_log": arr("L1_attn_A_log"), "d_par": arr("L1_attn_D_param"),
        "gate1_t": arr("L1_ffn_gate_w", 1, 0),
        "wg1": arr("L1_ffn_w_gate"), "wu1": arr("L1_ffn_w_up"), "wd1": arr("L1_ffn_w_down"),
        "shg_t": arr("L1_ffn_sh_gate", 1, 0), "shu_t": arr("L1_ffn_sh_up", 1, 0),
        "shd_t": arr("L1_ffn_sh_down", 1, 0),
    }
    nc = bacc.Bacc("TRN2", target_bir_lowering=False, num_devices=1)
    args = [nc.dram_tensor(f"in_{n}", a.shape, mybir.dt.from_np(a.dtype), kind="ExternalInput").ap()
            for n, a in arrays.items()]
    args.append(nc.dram_tensor("out_rows", (ROWS, D), F32, kind="ExternalOutput").ap())
    build(nc, *args)
    r = run_bass_kernel_spmd(nc, [{f"in_{n}": a for n, a in arrays.items()}], core_ids=[0])
    return r.results[0]["out_rows"][0:N].reshape(B, L, D)
```
